# Optimizing a Trainium2 kernel written in Bass

```python
import numpy as np
import jax
import jax.numpy as jnp

def _softmax(x, axis=-1):
    return jax.nn.softmax(x, axis=axis)

def _gelu(x):
    return jax.nn.gelu(x, approximate=True)

def _silu(x):
    return jax.nn.silu(x)

def _sigmoid(x):
    return jax.nn.sigmoid(x)

def _layernorm(x, axis=-1, eps=1e-05):
    m = jnp.mean(x, axis=axis, keepdims=True)
    v = jnp.var(x, axis=axis, keepdims=True)
    return (x - m) / jnp.sqrt(v + eps)

def _scatter_add(tgt, idx, src, axis=0):
    return tgt.at[idx].add(src)

def _segment_sum(src, seg, n):
    return jax.ops.segment_sum(src, seg, n)
kernel_name = 'mk_macaron_d1_jaxref_r8_20c648'

def setup_inputs(seed: int=0):
    np.random.seed(seed)
    _w = jnp.asarray

    def _L0_attn_setup():
        import jax, jax.numpy as jnp
        import numpy as np
        B, N, C, D = (4, 512, 128, 32)
        EPS = 1e-15
        PAD_VAL = 1.0
        key = jax.random.key(seed)
        k1, k2, k3 = jax.random.split(key, 3)
        x = jax.random.normal(k1, (B, N, C), dtype=jnp.float32)
        W_qkv = jax.random.normal(k2, (3 * C, C), dtype=jnp.float32) * 0.02
        W_proj = jax.random.normal(k3, (C, C), dtype=jnp.float32) * 0.02
        b_proj = jnp.zeros((C,), dtype=jnp.float32)
        return {'x': x, 'W_qkv': W_qkv, 'W_proj': W_proj, 'b_proj': b_proj}
    _L0_attn_in = _L0_attn_setup()

    def _L0_ffn_setup():
        import jax, jax.numpy as jnp
        import numpy as np
        B, S, H = (4, 256, 128)
        F = 512
        E = 8
        JITTER_EPS = 0.01

        def _sparse_mixer_top2(scores, jitter_eps):
            vals, idx = jax.lax.top_k(scores, 2)
            neg_inf = -jnp.inf
            m1 = vals[:, :1]
            factor1 = jnp.maximum(jnp.abs(scores), m1)
            mask1 = (m1 - scores) / factor1 > 2 * jitter_eps
            p1 = jax.nn.softmax(jnp.where(mask1, neg_inf, scores), axis=-1)
            mult1 = jnp.take_along_axis(p1, idx[:, :1], axis=-1)[:, 0]
            m2 = vals[:, 1:2]
            factor2 = jnp.maximum(jnp.abs(scores), m2)
            mask2 = (m2 - scores) / factor2 > 2 * jitter_eps
            top1_onehot = jnp.arange(scores.shape[-1])[None, :] == idx[:, :1]
            s2 = jnp.where(top1_onehot, neg_inf, scores)
            p2 = jax.nn.softmax(jnp.where(mask2, neg_inf, s2), axis=-1)
            mult2 = jnp.take_along_axis(p2, idx[:, 1:2], axis=-1)[:, 0]
            return (mult1, mult2, idx)
        key = jax.random.key(seed)
        k0, k1, k2, k3, k4 = jax.random.split(key, 5)
        hidden_states = jax.random.normal(k0, (B, S, H), dtype=jnp.float32)
        gate_w = jax.random.normal(k1, (E, H), dtype=jnp.float32) * 0.02
        w1 = jax.random.normal(k2, (E, F, H), dtype=jnp.float32) * 0.02
        w2 = jax.random.normal(k3, (E, H, F), dtype=jnp.float32) * 0.02
        w3 = jax.random.normal(k4, (E, F, H), dtype=jnp.float32) * 0.02
        return {'hidden_states': hidden_states, 'gate_w': gate_w, 'w1': w1, 'w2': w2, 'w3': w3}
    _L0_ffn_in = _L0_ffn_setup()
    _d = {'L0_attn_x': _L0_attn_in['x'], 'L0_attn_W_qkv': _L0_attn_in['W_qkv'], 'L0_attn_W_proj': _L0_attn_in['W_proj'], 'L0_attn_b_proj': _L0_attn_in['b_proj'], 'L0_ffn_gate_w': _L0_ffn_in['gate_w'], 'L0_ffn_w1': _L0_ffn_in['w1'], 'L0_ffn_w2': _L0_ffn_in['w2'], 'L0_ffn_w3': _L0_ffn_in['w3']}
    _x0 = _d['L0_attn_x']
    _d['L0_attn_x'] = jax.random.normal(jax.random.fold_in(jax.random.key(seed), 1), (8, 256, 128), dtype=_x0.dtype)
    del _x0
    return _d

def reference(L0_attn_x, L0_attn_W_qkv, L0_attn_W_proj, L0_attn_b_proj, L0_ffn_gate_w, L0_ffn_w1, L0_ffn_w2, L0_ffn_w3):

    def _L0_attn_ref(x, W_qkv, W_proj, b_proj):
        import jax, jax.numpy as jnp
        import numpy as np
        B, N, C, D = (4, 512, 128, 32)
        EPS = 1e-15
        PAD_VAL = 1.0
        Bx, Nx, Cx = x.shape
        h = Cx // D
        qkv = jnp.einsum('bnc,oc->bno', x, W_qkv)
        qkv = qkv.reshape(Bx, Nx, 3, Cx).transpose(0, 2, 3, 1)
        q, k, v = (qkv[:, 0], qkv[:, 1], qkv[:, 2])
        q = jax.nn.relu(q.reshape(Bx, h, D, Nx))
        k = jax.nn.relu(k.reshape(Bx, h, D, Nx)).transpose(0, 1, 3, 2)
        v = v.reshape(Bx, h, D, Nx)
        v = jnp.concatenate([v, jnp.full((Bx, h, 1, Nx), PAD_VAL, v.dtype)], axis=2)
        vk = jnp.einsum('bhdn,bhne->bhde', v, k)
        out = jnp.einsum('bhde,bhen->bhdn', vk, q)
        out = out[:, :, :-1] / (out[:, :, -1:] + EPS)
        out = out.reshape(Bx, Cx, Nx).transpose(0, 2, 1)
        return jnp.einsum('bnc,oc->bno', out, W_proj) + b_proj

    def _L0_ffn_ref(hidden_states, gate_w, w1, w2, w3):
        import jax, jax.numpy as jnp
        import numpy as np
        B, S, H = (4, 256, 128)
        F = 512
        E = 8
        JITTER_EPS = 0.01

        def _sparse_mixer_top2(scores, jitter_eps):
            vals, idx = jax.lax.top_k(scores, 2)
            neg_inf = -jnp.inf
            m1 = vals[:, :1]
            factor1 = jnp.maximum(jnp.abs(scores), m1)
            mask1 = (m1 - scores) / factor1 > 2 * jitter_eps
            p1 = jax.nn.softmax(jnp.where(mask1, neg_inf, scores), axis=-1)
            mult1 = jnp.take_along_axis(p1, idx[:, :1], axis=-1)[:, 0]
            m2 = vals[:, 1:2]
            factor2 = jnp.maximum(jnp.abs(scores), m2)
            mask2 = (m2 - scores) / factor2 > 2 * jitter_eps
            top1_onehot = jnp.arange(scores.shape[-1])[None, :] == idx[:, :1]
            s2 = jnp.where(top1_onehot, neg_inf, scores)
            p2 = jax.nn.softmax(jnp.where(mask2, neg_inf, s2), axis=-1)
            mult2 = jnp.take_along_axis(p2, idx[:, 1:2], axis=-1)[:, 0]
            return (mult1, mult2, idx)
        Bv, Sv, Hv = hidden_states.shape
        x = hidden_states.reshape(-1, Hv)
        scores = x @ gate_w.T
        mult1, mult2, idx = _sparse_mixer_top2(scores, JITTER_EPS)
        out = jnp.zeros_like(x)
        for e in range(E):
            w_tok = mult1 * (idx[:, 0] == e) + mult2 * (idx[:, 1] == e)
            h = jax.nn.silu(x @ w1[e].T) * (x @ w3[e].T)
            out = out + w_tok[:, None] * (h @ w2[e].T)
        return out.reshape(Bv, Sv, Hv)
    x = L0_attn_x
    x = x + 0.5 * _L0_ffn_ref(_layernorm(x, axis=-1), L0_ffn_gate_w, L0_ffn_w1, L0_ffn_w2, L0_ffn_w3)
    x = x + _L0_attn_ref(_layernorm(x, axis=-1), L0_attn_W_qkv, L0_attn_W_proj, L0_attn_b_proj)
    x = x + 0.5 * _L0_ffn_ref(_layernorm(x, axis=-1), L0_ffn_gate_w, L0_ffn_w1, L0_ffn_w2, L0_ffn_w3)
    return x

_drawn_inputs = setup_inputs


def setup_inputs(seed=0):
    import zlib

    import numpy as np

    out = dict(_drawn_inputs(seed))
    spreads = {'L0_attn_b_proj': (0.0, 0.1)}
    factors = {'L0_attn_W_qkv': 8.0,
     'L0_attn_W_proj': 8.0,
     'L0_ffn_gate_w': 4.053,
     'L0_ffn_w1': 3.529,
     'L0_ffn_w2': 3.522,
     'L0_ffn_w3': 3.511}
    for name, (base, spread) in spreads.items():
        noise = np.random.default_rng([zlib.crc32(name.encode()), seed]).standard_normal(out[name].shape)
        drawn = base * np.exp(spread * noise) if base else spread * noise
        out[name] = jnp.asarray(drawn.astype(out[name].dtype))
    for name, factor in factors.items():
        out[name] = (out[name] * factor).astype(out[name].dtype)
    return out
```

```python
from contextlib import ExitStack

import concourse.bass as bass
from concourse import mybir

F32 = mybir.dt.float32
F32R = mybir.dt.float32r
BF16 = mybir.dt.bfloat16
I32 = mybir.dt.int32
U32 = mybir.dt.uint32
ALU = mybir.AluOpType
ACT = mybir.ActivationFunctionType
AX = mybir.AxisListType.X

P = 128
C = 128
T = 2048
NT = T // P
NB = 8
TPB = NT // NB
TB = TPB * P
E = 8
F = 512
FC = F // P
K = 2
NG = 4
TG = NT // NG
BG = NB // NG
NS = (K * T + E * (P - 1)) // P
REG = T + P
SPARE = NS - K * T // P
XROWS = E * REG + SPARE * P
YROWS = K * T + (E + SPARE) * P
ROW = C + 2
HEADS = 4
D = C // HEADS
VW = C + HEADS
RING = 6
PR = 3
PB = 2
LOOPS = (NS - 3) // RING
assert NS == 39 and LOOPS * RING == NS - 3
EPS_LN = 1e-5
EPS_ATTN = 1e-15
JITTER = 0.02


class Count:

    def __init__(self):
        self.n = 0

    def next(self):
        self.n += 1
        return self.n


def build(nc, x, w_qkv, w_proj, b_proj, w_gate, w1, w3, w2, out):
    with ExitStack() as ctx:
        def sb(name, shape, dt=F32):
            return ctx.enter_context(nc.sbuf_tensor(name, shape, dt))

        def sem(name):
            return ctx.enter_context(nc.semaphore(name))

        sorted_rows = [nc.dram_tensor(f"sorted_rows{f}", [XROWS, ROW], F32, kind="Internal").ap() for f in range(2)]
        results = [nc.dram_tensor(f"results{f}", [YROWS, C], F32, kind="Internal").ap() for f in range(2)]
        results_kt = [r[0:K * T, :].rearrange("(k t p) c -> p k t c", k=K, p=P) for r in results]

        w13_raw = sb("w13_raw", [P, E, 2, F])
        w13_hi = sb("w13_hi", [P, E, 2, F], F32R)
        w13_lo = sb("w13_lo", [P, E, 2, F], F32R)
        w2_sb = sb("w2_sb", [P, E, FC, C])
        wqkv_sb = sb("wqkv_sb", [C, 3 * C])
        wproj_sb = sb("wproj_sb", [C, C])
        bproj_sb = sb("bproj_sb", [1, C])
        wgate_sb = sb("wgate_sb", [C, E])

        ident = sb("ident", [P, P])
        ones_f = sb("ones_f", [1, P])
        before = sb("before", [P, P], BF16)
        ones_b = sb("ones_b", [P, P], BF16)
        head_mask = sb("head_mask", [P, VW])
        iota_e = sb("iota_e", [P, E], I32)
        region = sb("region", [P, E], I32)
        thresholds = sb("thresholds", [1, E, NT], I32)
        iota_s = sb("iota_s", [1, NS], I32)
        iota_s128 = sb("iota_s128", [1, NS], I32)
        ones_e = sb("ones_e", [1, E])
        minus_half = sb("minus_half", [P, TPB])
        pad_rows = sb("pad_rows", [P, E + SPARE, ROW])

        X = sb("X", [P, NT, C])
        Y = w13_raw[:, 0:E // 2, :, :].rearrange("p e i f -> p (e i f)").rearrange("p (k t c) -> p k t c", k=K, c=C)
        xrow = sb("xrow", [P, K, NT, ROW])
        stats = sb("stats", [P, NT, 6])
        mv = sb("mv", [P, NT, 2])
        var_eps = sb("var_eps", [P, NT])
        rstd = sb("rstd", [P, NT])
        stats2 = sb("stats2", [P, NT, 6])
        mv2 = sb("mv2", [P, NT, 2])
        var_eps2 = sb("var_eps2", [P, NT])
        rstd2 = sb("rstd2", [P, NT])
        xnT = sb("xnT", [C, 2, TB])
        S = sb("S", [P, TG, E])
        Sabs = sb("Sabs", [P, TG, E])
        top = sb("top", [P, TG, 8])
        top_at = sb("top_at", [P, TG, 8], U32)
        gap = sb("gap", [P, TG, K, E])
        gap0 = sb("gap0", [P, TG, K, E])
        factor = sb("factor", [P, TG, K, E])
        keep = sb("keep", [P, TG, K, E])
        onehot = sb("onehot", [P, TG, K, E])
        expd = sb("expd", [P, TG, K, E])
        kept = sb("kept", [P, TG, K, E])
        denom = sb("denom", [P, TG, K])
        chosen = sb("chosen", [P, TG, E], BF16)
        chosen_sum = sb("chosen_sum", [P, E])
        carry = sb("carry", [P, NG + 1, E], BF16)
        place = sb("place", [P, TG, E])
        placed = sb("placed", [P, TG, K, E])
        slot = sb("slot", [P, NG, TG, K], I32)

        over = sb("over", [1, E, NT])
        tiles_of = sb("tiles_of", [1, E])
        tiles_end = sb("tiles_end", [1, E])
        past = sb("past", [1, NS, E])
        past_tiles = sb("past_tiles", [1, NS, E])
        expert_f = sb("expert_f", [1, NS])
        first_of = sb("first_of", [1, NS])
        row_a = sb("row_a", [1, NS])
        expert_tab = sb("expert_tab", [1, 2, NS], I32)
        row_tab = sb("row_tab", [1, 2, NS], I32)
        pad_tab = sb("pad_tab", [1, 2, E], I32)

        xg = sb("xg", [P, RING, ROW])
        xT_hi = sb("xT_hi", [C, PR, P], F32R)
        xT_lo = sb("xT_lo", [C, PR, P], F32R)
        silu = sb("silu", [P, PR, F])
        h = sb("h", [P, PR, F])
        hT = sb("hT", [P, PR, F])
        y = sb("y", [P, RING, C])

        xn2 = sb("xn2", [P, 2, TPB, C])
        xn2T = sb("xn2T", [C, 2, TB])
        qT = sb("qT", [C, 2, TB])
        kk = sb("kk", [P, 2, TPB, C])
        vv = sb("vv", [P, 2, TPB, VW])
        kv = sb("kv", [C, 2, VW])
        den = sb("den", [P, 2, TPB, HEADS])
        rden = sb("rden", [P, 2, TPB, HEADS])
        att = sb("att", [P, 2, TPB, C])
        attT = sb("attT", [C, 2, TB])

        banks = [ctx.enter_context(nc.psum_tensor(f"bank{i}", [P, 512], F32)) for i in range(8)]
        gate_ps = banks[0:PB]
        up_ps = banks[PB:2 * PB]
        hT_ps = banks[4]
        y_ps = banks[5][:, 0:C]
        xT_ps = banks[6][:, 0:P]
        xn2T_ps = banks[0][:, 0:TB]
        xnT_ps = banks[0][:, TB:2 * TB]
        q_ps = banks[1][:, 0:TB]
        kv_ps = banks[2][:, :].rearrange("p (t c) -> p t c", t=TPB)
        kvo_ps = banks[3][:, 0:VW]
        att_ps = banks[4][:, 0:TPB * VW].rearrange("p (t c) -> p t c", t=TPB)
        attT_ps = banks[5][:, 0:TB]
        proj_ps = banks[6][:, 0:TB].rearrange("p (t c) -> p t c", t=TPB)
        scores_ps = banks[7][:, 0:NT * E].rearrange("p (t e) -> p t e", t=NT)
        rank_ps = banks[7][:, NT * E:NT * E + TG * E].rearrange("p (t e) -> p t e", t=TG)
        count_ps = banks[7][:, 256:256 + E]

        x_loaded = [sem(f"x_loaded{g}") for g in range(NG)]
        wgate_loaded = sem("wgate_loaded")
        w13_loaded = [sem(f"w13_loaded{e}") for e in range(E)]
        w2_loaded = sem("w2_loaded")
        wattn_loaded = sem("wattn_loaded")
        y_loaded = [sem(f"y_loaded{b}") for b in range(NB)]
        consts_ready = sem("consts_ready")
        pool_own = sem("pool_own")
        dve_own = sem("dve_own")
        w13_hi_ready = sem("w13_hi_ready")
        w13_lo_ready = sem("w13_lo_ready")
        var_ready = sem("var_ready")
        rstd_ready = sem("rstd_ready")
        xn_ready = sem("xn_ready")
        xnT_ps_ready = sem("xnT_ps_ready")
        xnT_ready = sem("xnT_ready")
        scores_ready = sem("scores_ready")
        S_ready = sem("S_ready")
        gap_ready = sem("gap_ready")
        exp_ready = sem("exp_ready")
        chosen_ready = sem("chosen_ready")
        rank_ready = sem("rank_ready")
        place_ready = sem("place_ready")
        slot_ready = sem("slot_ready")
        carry_ready = sem("carry_ready")
        count_ready = sem("count_ready")
        tables_ready = sem("tables_ready")
        rows_scattered = sem("rows_scattered")
        pads_written = sem("pads_written")
        xg_loaded = [sem(f"xg_loaded{i}") for i in range(RING)]
        xT_ps_ready = sem("xT_ps_ready")
        xT_hi_ready = sem("xT_hi_ready")
        xT_lo_ready = sem("xT_lo_ready")
        gate_ps_ready = sem("gate_ps_ready")
        up_ps_ready = sem("up_ps_ready")
        silu_ready = sem("silu_ready")
        h_ready = sem("h_ready")
        hT_ps_ready = sem("hT_ps_ready")
        hT_ready = sem("hT_ready")
        y_ps_ready = sem("y_ps_ready")
        y_ready = sem("y_ready")
        y_scattered = [sem(f"y_scattered{i}") for i in range(RING)]
        x2_ready = sem("x2_ready")
        var2_ready = sem("var2_ready")
        rstd2_ready = sem("rstd2_ready")
        xn2_ready = sem("xn2_ready")
        xn2T_ps_ready = sem("xn2T_ps_ready")
        xn2T_ready = sem("xn2T_ready")
        q_ps_ready = sem("q_ps_ready")
        kv_ps_ready = sem("kv_ps_ready")
        q_ready = sem("q_ready")
        kv_in_ready = sem("kv_in_ready")
        kvo_ps_ready = sem("kvo_ps_ready")
        kv_ready = sem("kv_ready")
        att_ps_ready = sem("att_ps_ready")
        att_ready = sem("att_ready")
        attT_ps_ready = sem("attT_ps_ready")
        attT_ready = sem("attT_ready")
        proj_ps_ready = sem("proj_ps_ready")
        out_ready = sem("out_ready")
        out_stored = sem("out_stored")

        block = ctx.enter_context(nc.Block())

        LAG_QKV, LAG_KV, LAG_ATT, LAG_ATT_T, LAG_PROJ, LAG_XN_T, LAG_GATE = 1, 2, 3, 4, 5, 6, 7
        STEPS = NB + LAG_GATE

        def uses(slot_of_ring):
            return (NS - slot_of_ring + RING - 1) // RING

        def loop_tiles(engine, step):
            step(0, 0)
            with engine.Fori(0, LOOPS) as g:
                for c in range(1, RING + 1):
                    step(g, c)
            step(0, NS - 2)
            step(0, NS - 1)
            step(0, NS)

        @block.sync
        def _(sp):
            for g in range(NG):
                sp.dma_start(X[:, TG * g:TG * g + TG, :], x[:, TG * g:TG * g + TG, :]).then_inc(x_loaded[g], 16)
                if g == 0:
                    sp.dma_start(wgate_sb[:], w_gate).then_inc(wgate_loaded, 16)
            for e in range(E):
                sp.dma_start(w13_raw[:, e, 0, :], w1[:, e, :]).then_inc(w13_loaded[e], 16)
                sp.dma_start(w13_raw[:, e, 1, :], w3[:, e, :]).then_inc(w13_loaded[e], 16)
            sp.dma_start(w2_sb[:], w2).then_inc(w2_loaded, 16)
            sp.dma_start(wqkv_sb[:], w_qkv).then_inc(wattn_loaded, 16)
            sp.dma_start(wproj_sb[:], w_proj).then_inc(wattn_loaded, 16)
            sp.dma_start(bproj_sb[:], b_proj).then_inc(wattn_loaded, 16)
            sp.wait_ge(consts_ready, 2)
            for f in range(2):
                sp.dma_start(sorted_rows[f][E * REG:XROWS, :].rearrange("(n p) r -> p n r", p=P),
                             pad_rows[:, E:E + SPARE, :]).then_inc(pads_written, 16)

            for f in range(2):
                sp.wait_ge(tables_ready, 2 * f + 1)
                for e in range(E):
                    first = nc.sync.value_load(pad_tab[0:1, f, e:e + 1], min_val=0, max_val=E * REG - P)
                    sp.dma_start(sorted_rows[f][bass.ds(first, P), :], pad_rows[:, e, :]).then_inc(pads_written, 16)
                sp.wait_ge(tables_ready, 2 * f + 2)
                sp.wait_ge(rows_scattered, 16 * K * NT * (f + 1))
                sp.wait_ge(pads_written, 16 * (2 + E * (f + 1)))

                def load_tile(g, c, f=f):
                    s = c % RING
                    if not (isinstance(g, int) and c < RING):
                        sp.wait_ge(y_scattered[s], (g + (c // RING + f * uses(s))) * 16)
                    at = nc.sync.value_load(row_tab[0:1, f, bass.ds(g * RING + c, 1)], min_val=0, max_val=XROWS - P)
                    sp.dma_start(xg[:, s, :], sorted_rows[f][bass.ds(at, P), :]).then_inc(xg_loaded[s], 16)

                for c in range(RING):
                    load_tile(0, c)
                with sp.Fori(0, LOOPS - 1) as g:
                    for c in range(RING, 2 * RING):
                        load_tile(g, c)
                for c in range(LOOPS * RING, NS):
                    load_tile(0, c)

                for s in range(RING):
                    sp.wait_ge(y_scattered[s], 16 * uses(s) * (f + 1))
                for b in range(NB):
                    for k in range(K):
                        sp.dma_start(Y[:, k, TPB * b:TPB * (b + 1), :],
                                     results_kt[f][:, k, TPB * b:TPB * (b + 1), :]).then_inc(y_loaded[b], 16)
            for b in range(NB):
                sp.wait_ge(out_ready, b + 1)
                sp.dma_start(out[:, TPB * b:TPB * (b + 1), :], X[:, TPB * b:TPB * (b + 1), :]).then_inc(out_stored, 16)
            sp.wait_ge(out_stored, 16 * NB)

        @block.gpsimd
        def _(pool):
            own = Count()
            g = nc.gpsimd
            g.memset(minus_half[:], -0.5)
            g.memset(ident[:], 0.0).then_inc(pool_own, 1)
            pool.wait_ge(pool_own, own.next())
            g.affine_select(out=ident[:], in_=ident[:], compare_op=ALU.not_equal, fill=1.0, base=0,
                            pattern=[[-1, P]], channel_multiplier=1)
            g.memset(before[:], 1.0)
            g.memset(ones_b[:], 1.0)
            g.iota(iota_e[:], [[1, E]], base=0, channel_multiplier=0)
            g.iota(region[:], [[REG, E]], base=0, channel_multiplier=0)
            g.memset(carry[:, 0, :], 0.0)
            for k in range(K):
                at = xrow[:, k, :, C:C + 1].bitcast(I32)
                g.iota(at, [[P, NT], [0, 1]], base=k * T, channel_multiplier=1)
            g.memset(ones_f[:], 1.0).then_inc(pool_own, 1)
            pool.wait_ge(pool_own, own.next())
            g.affine_select(out=before[:], in_=before[:], compare_op=ALU.is_gt, fill=0.0, base=0,
                            pattern=[[1, P]], channel_multiplier=-1).then_inc(consts_ready, 1)

            def rstd_of(v, r, out_sem, b):
                s = slice(TPB * b, TPB * (b + 1))
                g.tensor_tensor(r[:, s], v[:, s], minus_half[:], ALU.pow).then_inc(out_sem, 1)

            def rstd_rows(f, b):
                pool.wait_ge(var_ready, NB * f + b + 1)
                rstd_of(var_eps, rstd, rstd_ready, b)

            def scatter(f, group, k, j):
                t = TG * group + j
                if j == 0 and k == 0:
                    pool.wait_ge(slot_ready, NG * f + group + 1)
                g.indirect_dma_start(
                    out=sorted_rows[f], out_offset=bass.IndirectOffsetOnAxis(ap=slot[:, group, j, k:k + 1], axis=0),
                    in_=xrow[:, k, t, :], in_offset=None).then_inc(rows_scattered, 16)

            def send_results(f):
                for i in range(NS):
                    s = i % RING
                    pool.wait_ge(y_ready, f * NS + i + 1)
                    g.indirect_dma_start(
                        out=results[f], out_offset=bass.IndirectOffsetOnAxis(ap=xg[:, s, C:C + 1].bitcast(I32), axis=0),
                        in_=y[:, s, :], in_offset=None).then_inc(y_scattered[s], 16)

            for b in range(NB):
                rstd_rows(0, b)
                if b == 1:
                    g.memset(head_mask[:], 1.0)
                    g.memset(pad_rows[:], 0.0)
                    g.iota(thresholds[:], [[0, E], [P, NT]], base=0, channel_multiplier=0)
                    g.iota(iota_s[:], [[1, NS]], base=0, channel_multiplier=0)
                    g.iota(iota_s128[:], [[P, NS]], base=0, channel_multiplier=0)
                    g.memset(ones_e[:], 1.0)
                    g.memset(vv[:, :, :, C:VW], 1.0).then_inc(pool_own, 1)
                    pool.wait_ge(pool_own, own.next())
                    g.iota(pad_rows[:, :, C:C + 1].bitcast(I32), [[P, E + SPARE], [0, 1]], base=K * T, channel_multiplier=1)
                    blocks = head_mask[:, 0:C].rearrange("p (h d) -> p h d", h=HEADS)
                    g.affine_select(out=blocks, in_=blocks, compare_op=ALU.is_ge, fill=0.0, base=0,
                                    pattern=[[-D, HEADS], [0, D]], channel_multiplier=1)
                    heads = head_mask[:, C:VW]
                    g.affine_select(out=heads, in_=heads, compare_op=ALU.is_ge, fill=0.0, base=0,
                                    pattern=[[-D, HEADS]], channel_multiplier=1).then_inc(pool_own, 1)
                    pool.wait_ge(pool_own, own.next())
                    g.affine_select(out=blocks, in_=blocks, compare_op=ALU.is_ge, fill=0.0, base=D - 1,
                                    pattern=[[D, HEADS], [0, D]], channel_multiplier=-1)
                    g.affine_select(out=heads, in_=heads, compare_op=ALU.is_ge, fill=0.0, base=D - 1,
                                    pattern=[[D, HEADS]], channel_multiplier=-1).then_inc(consts_ready, 1)
            for group in range(NG):
                for j in range(TG):
                    for k in range(K):
                        scatter(0, group, k, j)
            send_results(0)
            for s in range(STEPS + 4):
                pieces = []
                b = s - LAG_PROJ
                if 0 <= b < NB:
                    rstd_rows(1, b)
                if s < NB:
                    pool.wait_ge(var2_ready, s + 1)
                    rstd_of(var_eps2, rstd2, rstd2_ready, s)
                b = s - LAG_GATE - 2
                if 0 <= b < NB:
                    for j in range(TPB):
                        for k in range(K):
                            scatter(1, b // BG, k, TPB * (b % BG) + j)
            send_results(1)

        @block.scalar
        def _(act):
            def copy(out, in_, func=ACT.Copy):
                return nc.scalar.activation(out, in_, func)

            def xnT_copy(f, b):
                act.wait_ge(xnT_ps_ready, NB * f + b + 1)
                if b >= 2:
                    act.wait_ge(scores_ready, NB * f + b - 1)
                copy(xnT[:, b % 2, :], xnT_ps).then_inc(xnT_ready, 1)

            def scores_copy(f, group):
                act.wait_ge(scores_ready, NB * f + BG * (group + 1))
                if NG * f + group:
                    act.wait_ge(gap_ready, NG * f + group)
                part = scores_ps[:, TG * group:TG * (group + 1), :]
                copy(S[:], part)
                copy(Sabs[:], part, ACT.Abs).then_inc(S_ready, 1)

            def routing_exp(f, group):
                act.wait_ge(gap_ready, NG * f + group + 1)
                copy(expd[:], gap0[:], ACT.Exp).then_inc(exp_ready, 1)

            def experts(f):
                def x_hi(g, c):
                    act.wait_ge(xT_ps_ready, g * RING + (c + 1 + f * NS))
                    copy(xT_hi[:, c % PR, :], xT_ps).then_inc(xT_hi_ready, 1)

                def silus(g, c):
                    act.wait_ge(gate_ps_ready, g * RING + (c + 1 + f * NS))
                    copy(silu[:, c % PR, :], gate_ps[c % PB][:], ACT.Silu).then_inc(silu_ready, 1)

                def step(g, c):
                    last = isinstance(g, int)
                    if last and c == 0:
                        x_hi(0, 0)
                        x_hi(0, 1)
                        silus(0, 0)
                    if not last or c + 2 < NS:
                        x_hi(g, c + 2)
                    if not last or c + 1 < NS:
                        silus(g, c + 1)
                    if not last or c < NS:
                        act.wait_ge(hT_ps_ready, g * RING + (c + 1 + f * NS))
                        copy(hT[:, c % PR, :], hT_ps[:]).then_inc(hT_ready, 1)
                loop_tiles(act, step)

            for b in range(NB):
                xnT_copy(0, b)
                if b % BG == BG - 1:
                    scores_copy(0, b // BG)
                    routing_exp(0, b // BG)
            for e in range(E):
                act.wait_ge(w13_loaded[e], 32)
                copy(w13_hi[:, e, 0, :], w13_raw[:, e, 0, :])
                copy(w13_hi[:, e, 1, :], w13_raw[:, e, 1, :]).then_inc(w13_hi_ready, 1)
            experts(0)
            for s in range(STEPS + 2):
                b = s - LAG_GATE - 1
                if 0 <= b < NB and b % BG == BG - 1:
                    scores_copy(1, b // BG)
                    routing_exp(1, b // BG)
                b = s - LAG_XN_T
                if 0 <= b < NB:
                    xnT_copy(1, b)
                b = s - LAG_ATT_T
                if 0 <= b < NB:
                    act.wait_ge(attT_ps_ready, b + 1)
                    if b >= 2:
                        act.wait_ge(proj_ps_ready, b - 1)
                    copy(attT[:, b % 2, :], attT_ps).then_inc(attT_ready, 1)
                b = s - LAG_QKV
                if 0 <= b < NB:
                    act.wait_ge(q_ps_ready, b + 1)
                    if b >= 2:
                        act.wait_ge(att_ps_ready, b - 1)
                    copy(qT[:, b % 2, :], q_ps, ACT.Relu).then_inc(q_ready, 1)
                    act.wait_ge(kv_ps_ready, b + 1)
                    if b >= 2:
                        act.wait_ge(kvo_ps_ready, b - 1)
                    copy(kk[:, b % 2, :, :], kv_ps[:, :, 0:C], ACT.Relu)
                    copy(vv[:, b % 2, :, 0:C], kv_ps[:, :, C:2 * C]).then_inc(kv_in_ready, 1)
                b = s
                if b < NB:
                    act.wait_ge(xn2T_ps_ready, b + 1)
                    if b >= 2:
                        act.wait_ge(kv_ps_ready, b - 1)
                    copy(xn2T[:, b % 2, :], xn2T_ps).then_inc(xn2T_ready, 1)
            experts(1)

        @block.vector
        def _(dve):
            own = Count()
            v = nc.vector

            def stats_of(b, st, m, ve, ready):
                for t in range(TPB * b, TPB * (b + 1)):
                    last = v.bn_stats(st[:, t, :], X[:, t, :])
                last.then_inc(dve_own, 1)
                dve.wait_ge(dve_own, own.next())
                for t in range(TPB * b, TPB * (b + 1)):
                    last = v.bn_aggr(m[:, t, :], st[:, t, :])
                last.then_inc(dve_own, 1)
                dve.wait_ge(dve_own, own.next())
                s = slice(TPB * b, TPB * (b + 1))
                v.tensor_scalar(ve[:, s], m[:, s, 1], EPS_LN, None, ALU.add).then_inc(ready, 1)

            def normalise(out_of, b, m, r, ready):
                for t in range(TPB * b, TPB * (b + 1)):
                    last = v.tensor_scalar(out_of(t), X[:, t, :], m[:, t, 0:1], r[:, t:t + 1], ALU.subtract, ALU.mult)
                last.then_inc(ready, 1)

            def xn_rows(f, b):
                dve.wait_ge(rstd_ready, NB * f + b + 1)
                normalise(lambda t: xrow[:, 0, t, 0:C], b, mv, rstd, xn_ready)
                s = slice(TPB * b, TPB * (b + 1))
                dve.wait_ge(xn_ready, NB * f + b + 1)
                v.tensor_copy(xrow[:, 1, s, 0:C], xrow[:, 0, s, 0:C])

            def route_a(f, group):
                dve.wait_ge(S_ready, NG * f + group + 1)
                for t in range(TG):
                    last = v.max(top[:, t, :], S[:, t, :])
                last.then_inc(dve_own, 1)
                dve.wait_ge(dve_own, own.next())
                best = top[:, :, 0:K].unsqueeze(3).broadcast_to([P, TG, K, E])
                v.tensor_tensor(gap[:], S[:].unsqueeze(2).broadcast_to([P, TG, K, E]), best, ALU.subtract)
                v.tensor_tensor(factor[:], Sabs[:].unsqueeze(2).broadcast_to([P, TG, K, E]), best, ALU.max)
                for t in range(TG):
                    last = v.max_index(top_at[:, t, :], top[:, t, :], S[:, t, :])
                last.then_inc(dve_own, 1)
                dve.wait_ge(dve_own, own.next())
                v.tensor_scalar(gap0[:], gap[:], 0.0, None, ALU.min).then_inc(gap_ready, 1)
                v.tensor_tensor(onehot[:], top_at[:, :, 0:K].unsqueeze(3).broadcast_to([P, TG, K, E]),
                                iota_e[:].unsqueeze(1).unsqueeze(1).broadcast_to([P, TG, K, E]),
                                ALU.is_equal).then_inc(dve_own, 1)
                dve.wait_ge(dve_own, own.next())
                if NG * f + group:
                    dve.wait_ge(rank_ready, NG * f + group)
                v.tensor_tensor(chosen[:], onehot[:, :, 0, :], onehot[:, :, 1, :], ALU.add).then_inc(chosen_ready, 1)
                v.scalar_tensor_tensor(keep[:], factor[:], -JITTER, gap[:], ALU.mult, ALU.is_le).then_inc(dve_own, 1)
                dve.wait_ge(dve_own, own.next())
                v.tensor_tensor(keep[:, :, 1, :], keep[:, :, 1, :], onehot[:, :, 0, :], ALU.is_gt)
                v.tensor_reduce(chosen_sum[:], chosen[:].rearrange("p t e -> p e t"), AX, ALU.add).then_inc(dve_own, 1)
                dve.wait_ge(dve_own, own.next())
                v.tensor_tensor(carry[:, group + 1, :], carry[:, group, :], chosen_sum[:], ALU.add).then_inc(carry_ready, 1)
                dve.wait_ge(rank_ready, NG * f + group + 1)
                v.tensor_tensor(place[:], rank_ps, region[:].unsqueeze(1).broadcast_to([P, TG, E]),
                                ALU.add).then_inc(place_ready, 1)

            def route_b(f, group):
                dve.wait_ge(exp_ready, NG * f + group + 1)
                v.tensor_tensor(kept[:], keep[:], expd[:], ALU.mult).then_inc(dve_own, 1)
                dve.wait_ge(place_ready, NG * f + group + 1)
                dve.wait_ge(dve_own, own.next())
                v.tensor_reduce(denom[:], kept[:], AX, ALU.add).then_inc(dve_own, 1)
                dve.wait_ge(dve_own, own.next())
                v.tensor_tensor(placed[:], place[:].unsqueeze(2).broadcast_to([P, TG, K, E]), onehot[:],
                                ALU.mult).then_inc(dve_own, 1)
                weight = xrow[:, :, TG * group:TG * (group + 1), C + 1].rearrange("p k t -> p t k")
                v.reciprocal(weight, denom[:])
                dve.wait_ge(dve_own, own.next())
                with nc.allow_low_precision(reason="one whole number of each eight is not zero"):
                    v.tensor_reduce(slot[:, group, :, :], placed[:], AX, ALU.add).then_inc(slot_ready, 1)

            def tables(f):
                dve.wait_ge(count_ready, f + 1)
                dve.wait_ge(consts_ready, 2)
                v.tensor_tensor(pad_tab[:, f, :], count_ps[0:1, :], region[0:1, :], ALU.add).then_inc(tables_ready, 1)
                v.tensor_tensor(over[:], thresholds[:], count_ps[0:1, :].unsqueeze(2).broadcast_to([1, E, NT]),
                                ALU.is_lt).then_inc(dve_own, 1)
                dve.wait_ge(dve_own, own.next())
                v.tensor_reduce(tiles_of[:], over[:], AX, ALU.add).then_inc(dve_own, 1)
                dve.wait_ge(dve_own, own.next())
                v.tensor_tensor_scan(tiles_end[:], ones_e[:], tiles_of[:], 0.0, ALU.mult, ALU.add).then_inc(dve_own, 1)
                dve.wait_ge(dve_own, own.next())
                v.tensor_tensor(past[:], tiles_end[:].unsqueeze(1).broadcast_to([1, NS, E]),
                                iota_s[:].unsqueeze(2).broadcast_to([1, NS, E]), ALU.is_le).then_inc(dve_own, 1)
                dve.wait_ge(dve_own, own.next())
                v.tensor_tensor(past_tiles[:], past[:], tiles_of[:].unsqueeze(1).broadcast_to([1, NS, E]), ALU.mult)
                v.tensor_reduce(expert_f[:], past[:], AX, ALU.add).then_inc(dve_own, 1)
                dve.wait_ge(dve_own, own.next())
                v.tensor_reduce(first_of[:], past_tiles[:], AX, ALU.add)
                v.scalar_tensor_tensor(row_a[:], expert_f[:], float(REG), iota_s128[:], ALU.mult, ALU.add)
                v.tensor_scalar(expert_tab[:, f, :], expert_f[:], float(E - 1), None, ALU.min).then_inc(dve_own, 1)
                dve.wait_ge(dve_own, own.next())
                v.scalar_tensor_tensor(row_tab[:, f, :], first_of[:], float(-P), row_a[:], ALU.mult,
                                       ALU.add).then_inc(tables_ready, 1)

            def experts(f):
                def x_lo(g, c):
                    dve.wait_ge(xT_hi_ready, g * RING + (c + 1 + f * NS))
                    v.tensor_tensor(xT_lo[:, c % PR, :], xT_ps, xT_hi[:, c % PR, :].bitcast(F32),
                                    ALU.subtract).then_inc(xT_lo_ready, 1)

                def products(g, c):
                    dve.wait_ge(silu_ready, g * RING + (c + 1 + f * NS))
                    dve.wait_ge(up_ps_ready, g * RING + (c + 1 + f * NS))
                    v.tensor_tensor(h[:, c % PR, :], up_ps[c % PB][:], silu[:, c % PR, :], ALU.mult).then_inc(h_ready, 1)

                def step(g, c):
                    alone = isinstance(g, int)
                    if alone and c == 0:
                        x_lo(0, 0)
                        x_lo(0, 1)
                        products(0, 0)
                    if not alone or c + 2 < NS:
                        x_lo(g, c + 2)
                    if not alone or c + 1 < NS:
                        products(g, c + 1)
                    if not alone or c >= 1:
                        s = (c - 1) % RING
                        dve.wait_ge(y_ps_ready, g * RING + (c + f * NS))
                        if alone and c <= RING:
                            if f:
                                dve.wait_ge(y_scattered[s], 16 * f * uses(s))
                        elif alone:
                            dve.wait_ge(y_scattered[s], 16 * ((c - 1) // RING + f * uses(s)))
                        elif f:
                            dve.wait_ge(y_scattered[s], (g + ((c - 1) // RING + f * uses(s))) * 16)
                        v.tensor_scalar(y[:, s, :], y_ps, xg[:, s, C + 1:C + 2], None, ALU.mult).then_inc(y_ready, 1)
                loop_tiles(dve, step)

            def combine(f, b, ready):
                s = slice(TPB * b, TPB * (b + 1))
                dve.wait_ge(y_loaded[b], 32 * (f + 1))
                v.tensor_tensor(Y[:, 0, s, :], Y[:, 0, s, :], Y[:, 1, s, :], ALU.add).then_inc(dve_own, 1)
                dve.wait_ge(dve_own, own.next())
                v.scalar_tensor_tensor(X[:, s, :], Y[:, 0, s, :], 0.5, X[:, s, :], ALU.mult, ALU.add).then_inc(ready, 1)

            dve.wait_ge(consts_ready, 1)
            for b in range(NB):
                dve.wait_ge(x_loaded[b // BG], 16)
                stats_of(b, stats, mv, var_eps, var_ready)
                if b >= 1:
                    xn_rows(0, b - 1)
                if b >= 3 and b % BG == 1:
                    route_a(0, b // BG - 1)
                    route_b(0, b // BG - 1)
            xn_rows(0, NB - 1)
            route_a(0, NG - 1)
            route_b(0, NG - 1)
            tables(0)
            for e in range(E):
                dve.wait_ge(w13_hi_ready, e + 1)
                for i in range(2):
                    last = v.tensor_tensor(w13_lo[:, e, i, :], w13_raw[:, e, i, :], w13_hi[:, e, i, :].bitcast(F32),
                                           ALU.subtract)
                last.then_inc(w13_lo_ready, 1)
            experts(0)

            for s in range(STEPS + 3):
                b = s - LAG_GATE - 2
                if 0 <= b < NB and b % BG == BG - 1:
                    route_b(1, b // BG)
                b = s - LAG_GATE - 1
                if 0 <= b < NB and b % BG == BG - 1:
                    route_a(1, b // BG)
                b = s - LAG_PROJ
                if 0 <= b < NB:
                    t = slice(TPB * b, TPB * (b + 1))
                    dve.wait_ge(proj_ps_ready, b + 1)
                    v.tensor_tensor(X[:, t, :], proj_ps, X[:, t, :], ALU.add).then_inc(dve_own, 1)
                    dve.wait_ge(dve_own, own.next())
                    stats_of(b, stats, mv, var_eps, var_ready)
                b = s - LAG_ATT
                if 0 <= b < NB:
                    i = b % 2
                    dve.wait_ge(att_ps_ready, b + 1)
                    v.tensor_scalar(den[:, i, :, :], att_ps[:, :, C:VW], EPS_ATTN, None, ALU.add).then_inc(dve_own, 1)
                    dve.wait_ge(dve_own, own.next())
                    v.reciprocal(rden[:, i, :, :], den[:, i, :, :]).then_inc(dve_own, 1)
                    dve.wait_ge(dve_own, own.next())
                    if b >= 2:
                        dve.wait_ge(attT_ps_ready, b - 1)
                    v.tensor_tensor(att[:, i, :, :].rearrange("p t (h d) -> p t h d", h=HEADS),
                                    att_ps[:, :, 0:C].rearrange("p t (h d) -> p t h d", h=HEADS),
                                    rden[:, i, :, :].unsqueeze(3).broadcast_to([P, TPB, HEADS, D]),
                                    ALU.mult).then_inc(att_ready, 1)
                b = s - LAG_KV
                if 0 <= b < NB:
                    dve.wait_ge(kvo_ps_ready, b + 1)
                    if b >= 2:
                        dve.wait_ge(att_ps_ready, b - 1)
                    v.tensor_tensor(kv[:, b % 2, :], kvo_ps, head_mask[:], ALU.mult).then_inc(kv_ready, 1)
                b = s
                if b < NB:
                    combine(0, b, x2_ready)
                    dve.wait_ge(x2_ready, b + 1)
                    stats_of(b, stats2, mv2, var_eps2, var2_ready)
                b = s - LAG_PROJ
                if 0 <= b < NB:
                    xn_rows(1, b)
                b = s
                if b < NB:
                    dve.wait_ge(rstd2_ready, b + 1)
                    if b >= 2:
                        dve.wait_ge(xn2T_ps_ready, b - 1)
                    normalise(lambda t: xn2[:, b % 2, t % TPB, :], b, mv2, rstd2, xn2_ready)
            tables(1)
            experts(1)
            for b in range(NB):
                combine(1, b, out_ready)

        @block.tensor
        def _(pe):
            mm = nc.tensor.matmul

            def xn_transposes(f, b):
                pe.wait_ge(xn_ready, NB * f + b + 1)
                if NB * f + b:
                    pe.wait_ge(xnT_ready, NB * f + b)
                if f:
                    pe.wait_ge(xn2T_ready, min(b + LAG_XN_T, NB))
                for j in range(TPB):
                    last = nc.tensor.transpose(xnT_ps[:, j * P:(j + 1) * P], xrow[:, 0, TPB * b + j, 0:C], ident[:])
                last.then_inc(xnT_ps_ready, 1)

            def scores(f, b):
                pe.wait_ge(xnT_ready, NB * f + b + 1)
                done = NG * f + b // BG
                if done and b % BG == 0:
                    pe.wait_ge(S_ready, done)
                if done:
                    routed = done if f == 1 or b % BG == 1 else done - 1
                    if routed:
                        pe.wait_ge(place_ready, routed)
                for j in range(TPB):
                    last = mm(scores_ps[:, TPB * b + j, :], xnT[:, b % 2, j * P:(j + 1) * P], wgate_sb[:],
                              start=True, stop=True)
                last.then_inc(scores_ready, 1)

            def ranks(f, group):
                pe.wait_ge(chosen_ready, NG * f + group + 1)
                if group:
                    pe.wait_ge(carry_ready, (NG * f + group))
                mm(rank_ps, before[:], chosen[:], start=True, stop=False)
                for j in range(TG - 1):
                    mm(rank_ps[:, j + 1:TG, :], ones_b[:],
                       chosen[:, j:j + 1, :].broadcast_to([P, TG - 1 - j, E]), start=False, stop=False)
                mm(rank_ps, ones_b[:], carry[:, group:group + 1, :].broadcast_to([P, TG, E]),
                   start=False, stop=True).then_inc(rank_ready, 1)

            def counts(f):
                pe.wait_ge(carry_ready, NG * (f + 1))
                pe.wait_ge(place_ready, NG * (f + 1))
                mm(count_ps, ones_b[:], carry[:, NG, :], start=True, stop=True).then_inc(count_ready, 1)

            def experts(f):
                def expert_of(g, c):
                    return nc.tensor.value_load(expert_tab[0:1, f, bass.ds(g * RING + c, 1)], min_val=0, max_val=E - 1)

                def x_transpose(g, c):
                    s = c % RING
                    pe.wait_ge(xg_loaded[s], (g + (c // RING + 1 + f * uses(s))) * 16)
                    if not (isinstance(g, int) and c == 0 and f == 0):
                        pe.wait_ge(xT_lo_ready, g * RING + (c + f * NS))
                    nc.tensor.transpose(xT_ps, xg[:, s, 0:C], ident[:]).then_inc(xT_ps_ready, 1)

                def up(g, c):
                    s = c % PR
                    e = expert_of(g, c)
                    pe.wait_ge(xT_lo_ready, g * RING + (c + 1 + f * NS))
                    for i, (ps, ready) in enumerate(((gate_ps[c % PB], gate_ps_ready), (up_ps[c % PB], up_ps_ready))):
                        mm(ps[:], xT_hi[:, s, :], w13_hi[:, bass.ds(e, 1), i, :], start=True, stop=False)
                        mm(ps[:], xT_hi[:, s, :], w13_lo[:, bass.ds(e, 1), i, :], start=False, stop=False)
                        mm(ps[:], xT_lo[:, s, :], w13_hi[:, bass.ds(e, 1), i, :], start=False, stop=True)\
                            .then_inc(ready, 1)

                def down(g, c):
                    e = expert_of(g, c)
                    pe.wait_ge(hT_ready, g * RING + (c + 1 + f * NS))
                    if not (isinstance(g, int) and c == 0 and f == 0):
                        pe.wait_ge(y_ready, g * RING + (c + f * NS))
                    for j in range(FC):
                        last = mm(y_ps, hT[:, c % PR, j * P:(j + 1) * P], w2_sb[:, bass.ds(e, 1), j, :],
                                  start=(j == 0), stop=(j == FC - 1))
                    last.then_inc(y_ps_ready, 1)

                def step(g, c):
                    alone = isinstance(g, int)
                    if alone and c == 0:
                        x_transpose(0, 0)
                        x_transpose(0, 1)
                        up(0, 0)
                    if not alone or c + 2 < NS:
                        x_transpose(g, c + 2)
                    if not alone or c + 1 < NS:
                        up(g, c + 1)
                    if not alone or c >= 1:
                        down(g, c - 1)
                    if not alone or c < NS:
                        pe.wait_ge(h_ready, g * RING + (c + 1 + f * NS))
                        for j in range(FC):
                            last = nc.tensor.transpose(hT_ps[:, j * P:(j + 1) * P], h[:, c % PR, j * P:(j + 1) * P], ident[:])
                        last.then_inc(hT_ps_ready, 1)

                pe.wait_ge(tables_ready, 2 * f + 2)
                loop_tiles(pe, step)

            pe.wait_ge(consts_ready, 1)
            pe.wait_ge(wgate_loaded, 16)
            for b in range(NB):
                if b >= 3 and b % BG == 1:
                    ranks(0, b // BG - 1)
                xn_transposes(0, b)
                scores(0, b)
            ranks(0, NG - 1)
            counts(0)
            pe.wait_ge(w13_lo_ready, E)
            pe.wait_ge(w2_loaded, 16)
            experts(0)

            pe.wait_ge(wattn_loaded, 48)
            for s in range(STEPS + 2):
                b = s - LAG_GATE - 1
                if 0 <= b < NB and b % BG == BG - 1:
                    ranks(1, b // BG)
                b = s - LAG_GATE
                if 0 <= b < NB:
                    scores(1, b)
                b = s - LAG_XN_T
                if 0 <= b < NB:
                    xn_transposes(1, b)
                b = s - LAG_PROJ
                if 0 <= b < NB:
                    pe.wait_ge(attT_ready, b + 1)
                    if b:
                        pe.wait_ge(var_ready, NB + b)
                    for j in range(TPB):
                        mm(proj_ps[:, j, :], attT[:, b % 2, j * P:(j + 1) * P], wproj_sb[:], start=True, stop=False)
                        last = mm(proj_ps[:, j, :], ones_f[:], bproj_sb[:], start=False, stop=True)
                    last.then_inc(proj_ps_ready, 1)
                b = s - LAG_ATT_T
                if 0 <= b < NB:
                    pe.wait_ge(att_ready, b + 1)
                    if b:
                        pe.wait_ge(attT_ready, b)
                    for j in range(TPB):
                        last = nc.tensor.transpose(attT_ps[:, j * P:(j + 1) * P], att[:, b % 2, j, :], ident[:])
                    last.then_inc(attT_ps_ready, 1)
                b = s - LAG_ATT
                if 0 <= b < NB:
                    pe.wait_ge(q_ready, b + 1)
                    pe.wait_ge(kv_ready, b + 1)
                    if b:
                        pe.wait_ge(att_ready, b)
                    for j in range(TPB):
                        last = mm(att_ps[:, j, :], qT[:, b % 2, j * P:(j + 1) * P], kv[:, b % 2, :], start=True, stop=True)
                    last.then_inc(att_ps_ready, 1)
                b = s - LAG_KV
                if 0 <= b < NB:
                    pe.wait_ge(kv_in_ready, b + 1)
                    if b:
                        pe.wait_ge(kv_ready, b)
                    for j in range(TPB):
                        last = mm(kvo_ps, kk[:, b % 2, j, :], vv[:, b % 2, j, :], start=(j == 0), stop=(j == TPB - 1))
                    last.then_inc(kvo_ps_ready, 1)
                b = s - LAG_QKV
                if 0 <= b < NB:
                    pe.wait_ge(xn2T_ready, b + 1)
                    if b:
                        pe.wait_ge(q_ready, b)
                        pe.wait_ge(kv_in_ready, b)
                    mm(q_ps, wqkv_sb[:, 0:C], xn2T[:, b % 2, :], start=True, stop=True).then_inc(q_ps_ready, 1)
                    for j in range(TPB):
                        last = mm(kv_ps[:, j, :], xn2T[:, b % 2, j * P:(j + 1) * P], wqkv_sb[:, C:3 * C],
                                  start=True, stop=True)
                    last.then_inc(kv_ps_ready, 1)
                b = s
                if b < NB:
                    pe.wait_ge(xn2_ready, b + 1)
                    if b:
                        pe.wait_ge(xn2T_ready, b)
                    if b >= LAG_XN_T:
                        pe.wait_ge(xnT_ready, NB + b - LAG_XN_T + 1)
                    for j in range(TPB):
                        last = nc.tensor.transpose(xn2T_ps[:, j * P:(j + 1) * P], xn2[:, b % 2, j, :], ident[:])
                    last.then_inc(xn2T_ps_ready, 1)
            counts(1)
            experts(1)


def kernel(L0_attn_x, L0_attn_W_qkv, L0_attn_W_proj, L0_attn_b_proj, L0_ffn_gate_w, L0_ffn_w1, L0_ffn_w2, L0_ffn_w3):
    import numpy as np
    import concourse.bacc as bacc
    from concourse.bass_utils import run_bass_kernel_spmd

    def laid(a):
        return np.ascontiguousarray(a)

    inputs = {
        "x": laid(np.asarray(L0_attn_x).reshape(NT, P, C).transpose(1, 0, 2)),
        "w_qkv": laid(np.asarray(L0_attn_W_qkv).T),
        "w_proj": laid(np.asarray(L0_attn_W_proj).T),
        "b_proj": laid(np.asarray(L0_attn_b_proj).reshape(1, C)),
        "w_gate": laid(np.asarray(L0_ffn_gate_w).T),
        "w1": laid(np.asarray(L0_ffn_w1).transpose(2, 0, 1)),
        "w3": laid(np.asarray(L0_ffn_w3).transpose(2, 0, 1)),
        "w2": laid(np.asarray(L0_ffn_w2).transpose(2, 0, 1).reshape(FC, P, E, C).transpose(1, 2, 0, 3)),
    }
    nc = bacc.Bacc("TRN2", target_bir_lowering=False, num_devices=1)
    args = [nc.dram_tensor(f"{name}_in", a.shape, F32, kind="ExternalInput").ap() for name, a in inputs.items()]
    out = nc.dram_tensor("out", (P, NT, C), F32, kind="ExternalOutput").ap()
    build(nc, *args, out)
    r = run_bass_kernel_spmd(nc, [{f"{name}_in": a for name, a in inputs.items()}], core_ids=[0])
    return np.ascontiguousarray(r.results[0]["out"].transpose(1, 0, 2)).reshape(NB, TB, C)
```

```python
from contextlib import ExitStack

import concourse.bass as bass
from concourse import mybir

F32 = mybir.dt.float32
F32R = mybir.dt.float32r
BF16 = mybir.dt.bfloat16
I32 = mybir.dt.int32
U32 = mybir.dt.uint32
ALU = mybir.AluOpType
ACT = mybir.ActivationFunctionType
AX = mybir.AxisListType.X

P = 128
C = 128
T = 2048
NT = T // P
NB = 8
TPB = NT // NB
TB = TPB * P
E = 8
F = 512
FC = F // P
K = 2
NG = 4
TG = NT // NG
BG = NB // NG
NS = (K * T + E * (P - 1)) // P
REG = T + P
SPARE = NS - K * T // P
XROWS = E * REG + SPARE * P
YROWS = K * T + (E + SPARE) * P
ROW = C + 2
HEADS = 4
D = C // HEADS
VW = C + HEADS
RING = 6
PR = 3
PB = 2
LOOPS = (NS - 3) // RING
QB = 4
assert NS == 39 and LOOPS * RING == NS - 3
EPS_LN = 1e-5
EPS_ATTN = 1e-15
JITTER = 0.02


class Count:

    def __init__(self):
        self.n = 0

    def next(self):
        self.n += 1
        return self.n


def build(nc, x, w_qkv, w_proj, b_proj, w_gate, w1, w3, w2, out):
    with ExitStack() as ctx:
        def sb(name, shape, dt=F32):
            return ctx.enter_context(nc.sbuf_tensor(name, shape, dt))

        def sem(name):
            return ctx.enter_context(nc.semaphore(name))

        sorted_rows = [nc.dram_tensor(f"sorted_rows{f}", [XROWS, ROW], F32, kind="Internal").ap() for f in range(2)]
        results = [nc.dram_tensor(f"results{f}", [YROWS, C], F32, kind="Internal").ap() for f in range(2)]
        results_kt = [r[0:K * T, :].rearrange("(k t p) c -> p k t c", k=K, p=P) for r in results]

        w13_raw = sb("w13_raw", [P, E, 2, F])
        w13_hi = sb("w13_hi", [P, E, 2, F], F32R)
        w13_lo = sb("w13_lo", [P, E, 2, F], F32R)
        w2_sb = sb("w2_sb", [P, E, FC, C])
        wqkv_sb = sb("wqkv_sb", [C, 3 * C])
        wproj_sb = sb("wproj_sb", [C, C])
        bproj_sb = sb("bproj_sb", [1, C])
        wgate_sb = sb("wgate_sb", [C, E])

        ident = sb("ident", [P, P])
        ones_f = sb("ones_f", [1, P])
        before = sb("before", [P, P], BF16)
        ones_b = sb("ones_b", [P, P], BF16)
        head_mask = sb("head_mask", [P, VW])
        iota_e = sb("iota_e", [P, E], I32)
        region = sb("region", [P, E], I32)
        thresholds = sb("thresholds", [1, E, NT], I32)
        iota_s = sb("iota_s", [1, NS], I32)
        iota_s128 = sb("iota_s128", [1, NS], I32)
        ones_e = sb("ones_e", [1, E])
        minus_half = sb("minus_half", [P, TG])
        pad_rows = sb("pad_rows", [P, E + SPARE, ROW])

        X = sb("X", [P, NT, C])
        Y = w13_raw[:, 0:E // 2, :, :].rearrange("p e i f -> p (e i f)").rearrange("p (k t c) -> p k t c", k=K, c=C)
        xrow = sb("xrow", [P, K, NT, ROW])
        stats = sb("stats", [P, NT, 6])
        mv = sb("mv", [P, NT, 2])
        var_eps = sb("var_eps", [P, NT])
        rstd = sb("rstd", [P, NT])
        stats2 = sb("stats2", [P, NT, 6])
        mv2 = sb("mv2", [P, NT, 2])
        var_eps2 = sb("var_eps2", [P, NT])
        rstd2 = sb("rstd2", [P, NT])
        xnT = sb("xnT", [C, 2, TB])
        S = sb("S", [P, TG, E])
        Sabs = sb("Sabs", [P, TG, E])
        top = sb("top", [P, TG, 8])
        top_at = sb("top_at", [P, TG, 8], U32)
        gap = sb("gap", [P, TG, K, E])
        gap0 = sb("gap0", [P, TG, K, E])
        factor = sb("factor", [P, TG, K, E])
        keep = sb("keep", [P, TG, K, E])
        onehot = sb("onehot", [P, TG, K, E])
        expd = sb("expd", [P, TG, K, E])
        kept = sb("kept", [P, TG, K, E])
        denom = sb("denom", [P, TG, K])
        chosen = sb("chosen", [P, TG, E], BF16)
        chosen_sum = sb("chosen_sum", [P, E])
        carry = sb("carry", [P, NG + 1, E], BF16)
        place = sb("place", [P, TG, E])
        placed = sb("placed", [P, TG, K, E])
        slot = sb("slot", [P, NG, TG, K], I32)

        over = sb("over", [1, E, NT])
        tiles_of = sb("tiles_of", [1, E])
        tiles_end = sb("tiles_end", [1, E])
        past = sb("past", [1, NS, E])
        past_tiles = sb("past_tiles", [1, NS, E])
        expert_f = sb("expert_f", [1, NS])
        first_of = sb("first_of", [1, NS])
        row_a = sb("row_a", [1, NS])
        expert_tab = sb("expert_tab", [1, 2, NS], I32)
        row_tab = sb("row_tab", [1, 2, NS], I32)
        pad_tab = sb("pad_tab", [1, 2, E], I32)

        xg = sb("xg", [P, RING, ROW])
        result_row = sb("result_row", [P, RING], I32)
        row_weight = sb("row_weight", [P, RING])
        xT_hi = sb("xT_hi", [C, PR, P], F32R)
        xT_lo = sb("xT_lo", [C, PR, P], F32R)
        silu = sb("silu", [P, PR, F])
        h = sb("h", [P, PR, F])
        hT = sb("hT", [P, PR, F])
        y = sb("y", [P, RING, C])

        xn2 = sb("xn2", [P, 2, TPB, C])
        xn2T = sb("xn2T", [C, 2, TB])
        qT = sb("qT", [C, QB, TB])
        kk = sb("kk", [P, 2, TPB, C])
        vv = sb("vv", [P, 2, TPB, VW])
        kv = sb("kv", [C, 2, VW])
        den = sb("den", [P, 2, TPB, HEADS])
        rden = sb("rden", [P, 2, TPB, HEADS])
        att = sb("att", [P, 2, TPB, C])
        attT = sb("attT", [C, 2, TB])

        banks = [ctx.enter_context(nc.psum_tensor(f"bank{i}", [P, 512], F32)) for i in range(8)]
        gate_ps = banks[0:PB]
        up_ps = banks[PB:2 * PB]
        hT_ps = banks[4]
        y_ps = banks[5][:, 0:C]
        xT_ps = banks[6][:, 0:P]
        xn2T_ps = banks[0][:, 0:TB]
        xnT_ps = banks[0][:, TB:2 * TB]
        q_ps = banks[1][:, 0:TB]
        kv_ps = banks[2][:, :].rearrange("p (t c) -> p t c", t=TPB)
        kvo_ps = banks[3][:, 0:VW]
        att_ps = banks[4][:, 0:TPB * VW].rearrange("p (t c) -> p t c", t=TPB)
        attT_ps = banks[5][:, 0:TB]
        proj_ps = banks[6][:, 0:TB].rearrange("p (t c) -> p t c", t=TPB)
        scores_ps = banks[7][:, 0:NT * E].rearrange("p (t e) -> p t e", t=NT)
        rank_ps = banks[7][:, NT * E:NT * E + TG * E].rearrange("p (t e) -> p t e", t=TG)
        count_ps = banks[7][:, 256:256 + E]

        x_loaded = [sem(f"x_loaded{g}") for g in range(NG)]
        wgate_loaded = sem("wgate_loaded")
        w13_loaded = [sem(f"w13_loaded{e}") for e in range(E)]
        w2_loaded = sem("w2_loaded")
        wattn_loaded = sem("wattn_loaded")
        y_loaded = [sem(f"y_loaded{b}") for b in range(NB)]
        consts_ready = sem("consts_ready")
        pool_own = sem("pool_own")
        dve_own = sem("dve_own")
        w13_hi_ready = sem("w13_hi_ready")
        w13_lo_ready = sem("w13_lo_ready")
        var_ready = sem("var_ready")
        rstd_ready = sem("rstd_ready")
        xn_ready = sem("xn_ready")
        xnT_ps_ready = sem("xnT_ps_ready")
        xnT_ready = sem("xnT_ready")
        scores_ready = sem("scores_ready")
        S_ready = sem("S_ready")
        gap_ready = sem("gap_ready")
        exp_ready = sem("exp_ready")
        chosen_ready = sem("chosen_ready")
        rank_ready = sem("rank_ready")
        place_ready = sem("place_ready")
        slot_ready = sem("slot_ready")
        carry_ready = sem("carry_ready")
        count_ready = sem("count_ready")
        tables_ready = sem("tables_ready")
        rows_scattered = sem("rows_scattered")
        pads_written = sem("pads_written")
        xg_loaded = [sem(f"xg_loaded{i}") for i in range(RING)]
        xT_ps_ready = sem("xT_ps_ready")
        xT_hi_ready = sem("xT_hi_ready")
        xT_lo_ready = sem("xT_lo_ready")
        gate_ps_ready = sem("gate_ps_ready")
        up_ps_ready = sem("up_ps_ready")
        silu_ready = sem("silu_ready")
        h_ready = sem("h_ready")
        hT_ps_ready = sem("hT_ps_ready")
        hT_ready = sem("hT_ready")
        y_ps_ready = sem("y_ps_ready")
        y_ready = sem("y_ready")
        y_scattered = [sem(f"y_scattered{i}") for i in range(RING)]
        x2_ready = sem("x2_ready")
        var2_ready = sem("var2_ready")
        rstd2_ready = sem("rstd2_ready")
        xn2_ready = sem("xn2_ready")
        xn2T_ps_ready = sem("xn2T_ps_ready")
        xn2T_ready = sem("xn2T_ready")
        q_ps_ready = sem("q_ps_ready")
        kv_ps_ready = sem("kv_ps_ready")
        q_ready = sem("q_ready")
        kv_in_ready = sem("kv_in_ready")
        kvo_ps_ready = sem("kvo_ps_ready")
        kv_ready = sem("kv_ready")
        att_ps_ready = sem("att_ps_ready")
        att_ready = sem("att_ready")
        attT_ps_ready = sem("attT_ps_ready")
        attT_ready = sem("attT_ready")
        proj_ps_ready = sem("proj_ps_ready")
        x3_ready = sem("x3_ready")
        out_ready = sem("out_ready")
        out_stored = sem("out_stored")

        block = ctx.enter_context(nc.Block())

        LAG_XN2, LAG_XN2_T, LAG_QKV, LAG_KVO, LAG_KV, LAG_ATT, LAG_DIV, LAG_ATT_T, LAG_PROJ = 1, 2, 3, 4, 5, 6, 7, 8, 9
        LAG_X3, LAG_XN, LAG_XN_T, LAG_GATE, LAG_ROUTE, LAG_PLACE = 10, 11, 12, 13, 14, 15
        STEPS = NB + LAG_PLACE

        def uses(slot_of_ring):
            return (NS - slot_of_ring + RING - 1) // RING

        def loop_tiles(engine, step):
            step(0, 0)
            with engine.Fori(0, LOOPS) as g:
                for c in range(1, RING + 1):
                    step(g, c)
            step(0, NS - 2)
            step(0, NS - 1)
            step(0, NS)

        @block.sync
        def _(sp):
            for g in range(NG):
                sp.dma_start(X[:, TG * g:TG * g + TG, :], x[:, TG * g:TG * g + TG, :]).then_inc(x_loaded[g], 16)
                if g == 0:
                    sp.dma_start(wgate_sb[:], w_gate).then_inc(wgate_loaded, 16)
            for e in range(E):
                sp.dma_start(w13_raw[:, e, 0, :], w1[:, e, :]).then_inc(w13_loaded[e], 16)
                sp.dma_start(w13_raw[:, e, 1, :], w3[:, e, :]).then_inc(w13_loaded[e], 16)
            sp.dma_start(w2_sb[:], w2).then_inc(w2_loaded, 16)
            sp.dma_start(wqkv_sb[:], w_qkv).then_inc(wattn_loaded, 16)
            sp.dma_start(wproj_sb[:], w_proj).then_inc(wattn_loaded, 16)
            sp.dma_start(bproj_sb[:], b_proj).then_inc(wattn_loaded, 16)
            sp.wait_ge(consts_ready, 2)
            for f in range(2):
                sp.dma_start(sorted_rows[f][E * REG:XROWS, :].rearrange("(n p) r -> p n r", p=P),
                             pad_rows[:, E:E + SPARE, :]).then_inc(pads_written, 16)

            for f in range(2):
                sp.wait_ge(tables_ready, 2 * f + 1)
                for e in range(E):
                    first = nc.sync.value_load(pad_tab[0:1, f, e:e + 1], min_val=0, max_val=E * REG - P)
                    sp.dma_start(sorted_rows[f][bass.ds(first, P), :], pad_rows[:, e, :]).then_inc(pads_written, 16)
                sp.wait_ge(tables_ready, 2 * f + 2)
                sp.wait_ge(rows_scattered, 16 * K * NT * (f + 1))
                sp.wait_ge(pads_written, 16 * (2 + E * (f + 1)))

                def load_tile(g, c, f=f):
                    s = c % RING
                    if not (isinstance(g, int) and c < RING):
                        sp.wait_ge(xT_lo_ready, g * RING + (c - RING + 1 + f * NS))
                    at = nc.sync.value_load(row_tab[0:1, f, bass.ds(g * RING + c, 1)], min_val=0, max_val=XROWS - P)
                    sp.dma_start(xg[:, s, :], sorted_rows[f][bass.ds(at, P), :]).then_inc(xg_loaded[s], 16)

                for c in range(RING):
                    load_tile(0, c)
                with sp.Fori(0, LOOPS - 1) as g:
                    for c in range(RING, 2 * RING):
                        load_tile(g, c)
                for c in range(LOOPS * RING, NS):
                    load_tile(0, c)

                for s in range(RING):
                    sp.wait_ge(y_scattered[s], 16 * uses(s) * (f + 1))
                for b in range(NB):
                    for k in range(K):
                        sp.dma_start(Y[:, k, TPB * b:TPB * (b + 1), :],
                                     results_kt[f][:, k, TPB * b:TPB * (b + 1), :]).then_inc(y_loaded[b], 16)
            for b in range(NB):
                sp.wait_ge(out_ready, b + 1)
                sp.dma_start(out[:, TPB * b:TPB * (b + 1), :], X[:, TPB * b:TPB * (b + 1), :]).then_inc(out_stored, 16)
            sp.wait_ge(out_stored, 16 * NB)

        @block.gpsimd
        def _(pool):
            own = Count()
            g = nc.gpsimd
            g.memset(minus_half[:], -0.5)
            g.memset(ident[:], 0.0).then_inc(pool_own, 1)
            pool.wait_ge(pool_own, own.next())
            g.affine_select(out=ident[:], in_=ident[:], compare_op=ALU.not_equal, fill=1.0, base=0,
                            pattern=[[-1, P]], channel_multiplier=1)
            g.memset(before[:], 1.0)
            g.memset(ones_b[:], 1.0)
            g.iota(iota_e[:], [[1, E]], base=0, channel_multiplier=0)
            g.iota(region[:], [[REG, E]], base=0, channel_multiplier=0)
            g.memset(carry[:, 0, :], 0.0)
            for k in range(K):
                g.iota(xrow[:, k, :, C:C + 1], [[P, NT], [0, 1]], base=k * T, channel_multiplier=1,
                       allow_small_or_imprecise_dtypes=True)
            g.memset(ones_f[:], 1.0).then_inc(pool_own, 1)
            pool.wait_ge(pool_own, own.next())
            g.affine_select(out=before[:], in_=before[:], compare_op=ALU.is_gt, fill=0.0, base=0,
                            pattern=[[1, P]], channel_multiplier=-1).then_inc(consts_ready, 1)

            def rstd_of(s, v, r, out_sem):
                g.tensor_tensor(r[:, s], v[:, s], minus_half[:, 0:s.stop - s.start], ALU.pow).then_inc(out_sem, 1)

            def scatter(f, group, k, j):
                t = TG * group + j
                if j == 0 and k == 0:
                    pool.wait_ge(slot_ready, NG * f + group + 1)
                g.indirect_dma_start(
                    out=sorted_rows[f], out_offset=bass.IndirectOffsetOnAxis(ap=slot[:, group, j, k:k + 1], axis=0),
                    in_=xrow[:, k, t, :], in_offset=None).then_inc(rows_scattered, 16)

            def send_results(f):
                for i in range(NS):
                    s = i % RING
                    pool.wait_ge(y_ready, f * NS + i + 1)
                    g.indirect_dma_start(
                        out=results[f], out_offset=bass.IndirectOffsetOnAxis(ap=result_row[:, s:s + 1], axis=0),
                        in_=y[:, s, :], in_offset=None).then_inc(y_scattered[s], 16)

            for group in range(NG):
                pool.wait_ge(var_ready, group + 1)
                rstd_of(slice(TG * group, TG * (group + 1)), var_eps, rstd, rstd_ready)
            g.memset(head_mask[:], 1.0)
            g.memset(pad_rows[:], 0.0)
            g.iota(thresholds[:], [[0, E], [P, NT]], base=0, channel_multiplier=0)
            g.iota(iota_s[:], [[1, NS]], base=0, channel_multiplier=0)
            g.iota(iota_s128[:], [[P, NS]], base=0, channel_multiplier=0)
            g.memset(ones_e[:], 1.0)
            g.memset(vv[:, :, :, C:VW], 1.0).then_inc(pool_own, 1)
            pool.wait_ge(pool_own, own.next())
            g.iota(pad_rows[:, :, C:C + 1], [[P, E + SPARE], [0, 1]], base=K * T, channel_multiplier=1,
                   allow_small_or_imprecise_dtypes=True)
            blocks = head_mask[:, 0:C].rearrange("p (h d) -> p h d", h=HEADS)
            g.affine_select(out=blocks, in_=blocks, compare_op=ALU.is_ge, fill=0.0, base=0,
                            pattern=[[-D, HEADS], [0, D]], channel_multiplier=1)
            heads = head_mask[:, C:VW]
            g.affine_select(out=heads, in_=heads, compare_op=ALU.is_ge, fill=0.0, base=0,
                            pattern=[[-D, HEADS]], channel_multiplier=1).then_inc(pool_own, 1)
            pool.wait_ge(pool_own, own.next())
            g.affine_select(out=blocks, in_=blocks, compare_op=ALU.is_ge, fill=0.0, base=D - 1,
                            pattern=[[D, HEADS], [0, D]], channel_multiplier=-1)
            g.affine_select(out=heads, in_=heads, compare_op=ALU.is_ge, fill=0.0, base=D - 1,
                             pattern=[[D, HEADS]], channel_multiplier=-1).then_inc(consts_ready, 1)
            for group in range(NG):
                for j in range(TG):
                    for k in range(K):
                        scatter(0, group, k, j)
            send_results(0)
            for s in range(STEPS):
                b = s - LAG_X3
                if 0 <= b < NB:
                    pool.wait_ge(var_ready, NG + b + 1)
                    rstd_of(slice(TPB * b, TPB * (b + 1)), var_eps, rstd, rstd_ready)
                b = s
                if b < NB:
                    pool.wait_ge(var2_ready, b + 1)
                    rstd_of(slice(TPB * b, TPB * (b + 1)), var_eps2, rstd2, rstd2_ready)
                b = s - LAG_PLACE
                if 0 <= b < NB:
                    for n in range(TPB):
                        for k in range(K):
                            if b >= BG - 1:
                                t = TPB * (b - (BG - 1)) + n
                                scatter(1, t // TG, k, t % TG)
            for b in range(NB - (BG - 1), NB):
                for n in range(TPB):
                    for k in range(K):
                        t = TPB * b + n
                        scatter(1, t // TG, k, t % TG)
            send_results(1)

        @block.scalar
        def _(act):
            def copy(out, in_, func=ACT.Copy):
                return nc.scalar.activation(out, in_, func)

            def xnT_copy(f, b):
                act.wait_ge(xnT_ps_ready, NB * f + b + 1)
                if b >= 2:
                    act.wait_ge(scores_ready, NB * f + b - 1)
                copy(xnT[:, b % 2, :], xnT_ps).then_inc(xnT_ready, 1)

            def scores_copy(f, group):
                act.wait_ge(scores_ready, NB * f + BG * (group + 1))
                if NG * f + group:
                    act.wait_ge(gap_ready, NG * f + group)
                part = scores_ps[:, TG * group:TG * (group + 1), :]
                copy(S[:], part)
                copy(Sabs[:], part, ACT.Abs).then_inc(S_ready, 1)

            def routing_exp(f, group):
                act.wait_ge(gap_ready, NG * f + group + 1)
                copy(expd[:], gap0[:], ACT.Exp).then_inc(exp_ready, 1)

            def experts(f):
                def x_hi(g, c):
                    act.wait_ge(xT_ps_ready, g * RING + (c + 1 + f * NS))
                    copy(xT_hi[:, c % PR, :], xT_ps).then_inc(xT_hi_ready, 1)

                def silus(g, c):
                    act.wait_ge(gate_ps_ready, g * RING + (c + 1 + f * NS))
                    copy(silu[:, c % PR, :], gate_ps[c % PB][:], ACT.Silu).then_inc(silu_ready, 1)

                def step(g, c):
                    last = isinstance(g, int)
                    if last and c == 0:
                        x_hi(0, 0)
                        x_hi(0, 1)
                        silus(0, 0)
                    if not last or c + 2 < NS:
                        x_hi(g, c + 2)
                    if not last or c + 1 < NS:
                        silus(g, c + 1)
                    if not last or c < NS:
                        act.wait_ge(hT_ps_ready, g * RING + (c + 1 + f * NS))
                        copy(hT[:, c % PR, :], hT_ps[:]).then_inc(hT_ready, 1)
                loop_tiles(act, step)

            for b in range(NB):
                xnT_copy(0, b)
                if b % BG == BG - 1:
                    scores_copy(0, b // BG)
                    routing_exp(0, b // BG)
            for e in range(E):
                act.wait_ge(w13_loaded[e], 32)
                copy(w13_hi[:, e, 0, :], w13_raw[:, e, 0, :])
                copy(w13_hi[:, e, 1, :], w13_raw[:, e, 1, :]).then_inc(w13_hi_ready, 1)
            experts(0)
            for s in range(STEPS):
                b = s - LAG_GATE
                if 0 <= b < NB and b % BG == BG - 1:
                    scores_copy(1, b // BG)
                b = s - LAG_ROUTE
                if 0 <= b < NB and b % BG == BG - 1:
                    routing_exp(1, b // BG)
                b = s - LAG_XN_T
                if 0 <= b < NB:
                    xnT_copy(1, b)
                b = s - LAG_ATT_T
                if 0 <= b < NB:
                    act.wait_ge(attT_ps_ready, b + 1)
                    if b >= 2:
                        act.wait_ge(proj_ps_ready, b - 1)
                    copy(attT[:, b % 2, :], attT_ps).then_inc(attT_ready, 1)
                b = s - LAG_QKV
                if 0 <= b < NB:
                    act.wait_ge(q_ps_ready, b + 1)
                    if b >= QB:
                        act.wait_ge(att_ps_ready, b - QB + 1)
                    copy(qT[:, b % QB, :], q_ps, ACT.Relu).then_inc(q_ready, 1)
                    act.wait_ge(kv_ps_ready, b + 1)
                    if b >= 2:
                        act.wait_ge(kvo_ps_ready, b - 1)
                    copy(kk[:, b % 2, :, :], kv_ps[:, :, 0:C], ACT.Relu)
                    copy(vv[:, b % 2, :, 0:C], kv_ps[:, :, C:2 * C]).then_inc(kv_in_ready, 1)
                b = s - LAG_XN2_T
                if 0 <= b < NB:
                    act.wait_ge(xn2T_ps_ready, b + 1)
                    if b >= 2:
                        act.wait_ge(kv_ps_ready, b - 1)
                    copy(xn2T[:, b % 2, :], xn2T_ps).then_inc(xn2T_ready, 1)
            experts(1)

        @block.vector
        def _(dve):
            own = Count()
            v = nc.vector

            def stats_of(s, st, m, ve, ready):
                for t in range(s.start, s.stop):
                    last = v.bn_stats(st[:, t, :], X[:, t, :])
                last.then_inc(dve_own, 1)
                dve.wait_ge(dve_own, own.next())
                for t in range(s.start, s.stop):
                    last = v.bn_aggr(m[:, t, :], st[:, t, :])
                last.then_inc(dve_own, 1)
                dve.wait_ge(dve_own, own.next())
                v.tensor_scalar(ve[:, s], m[:, s, 1], EPS_LN, None, ALU.add).then_inc(ready, 1)

            def normalise(out_of, s, m, r, ready):
                for t in range(s.start, s.stop):
                    last = v.tensor_scalar(out_of(t), X[:, t, :], m[:, t, 0:1], r[:, t:t + 1], ALU.subtract, ALU.mult)
                last.then_inc(ready, 1)

            def xn_rows(s, n):
                dve.wait_ge(rstd_ready, n)
                normalise(lambda t: xrow[:, 0, t, 0:C], s, mv, rstd, xn_ready)

            def copy_rows(s, n):
                dve.wait_ge(xn_ready, n)
                v.tensor_copy(xrow[:, 1, s, 0:C], xrow[:, 0, s, 0:C])

            def route_a(f, group):
                dve.wait_ge(S_ready, NG * f + group + 1)
                for t in range(TG):
                    last = v.max(top[:, t, :], S[:, t, :])
                last.then_inc(dve_own, 1)
                dve.wait_ge(dve_own, own.next())
                best = top[:, :, 0:K].unsqueeze(3).broadcast_to([P, TG, K, E])
                v.tensor_tensor(gap[:], S[:].unsqueeze(2).broadcast_to([P, TG, K, E]), best, ALU.subtract)
                v.tensor_tensor(factor[:], Sabs[:].unsqueeze(2).broadcast_to([P, TG, K, E]), best, ALU.max)
                for t in range(TG):
                    last = v.max_index(top_at[:, t, :], top[:, t, :], S[:, t, :])
                last.then_inc(dve_own, 1)
                dve.wait_ge(dve_own, own.next())
                v.tensor_scalar(gap0[:], gap[:], 0.0, None, ALU.min).then_inc(gap_ready, 1)
                v.tensor_tensor(onehot[:], top_at[:, :, 0:K].unsqueeze(3).broadcast_to([P, TG, K, E]),
                                iota_e[:].unsqueeze(1).unsqueeze(1).broadcast_to([P, TG, K, E]),
                                ALU.is_equal).then_inc(dve_own, 1)
                dve.wait_ge(dve_own, own.next())
                if NG * f + group:
                    dve.wait_ge(rank_ready, NG * f + group)
                v.tensor_tensor(chosen[:], onehot[:, :, 0, :], onehot[:, :, 1, :], ALU.add).then_inc(chosen_ready, 1)
                v.scalar_tensor_tensor(keep[:], factor[:], -JITTER, gap[:], ALU.mult, ALU.is_le).then_inc(dve_own, 1)
                dve.wait_ge(dve_own, own.next())
                v.tensor_tensor(keep[:, :, 1, :], keep[:, :, 1, :], onehot[:, :, 0, :], ALU.is_gt)
                v.tensor_reduce(chosen_sum[:], chosen[:].rearrange("p t e -> p e t"), AX, ALU.add).then_inc(dve_own, 1)
                dve.wait_ge(dve_own, own.next())
                v.tensor_tensor(carry[:, group + 1, :], carry[:, group, :], chosen_sum[:], ALU.add).then_inc(carry_ready, 1)
                dve.wait_ge(rank_ready, NG * f + group + 1)
                v.tensor_tensor(place[:], rank_ps, region[:].unsqueeze(1).broadcast_to([P, TG, E]),
                                ALU.add).then_inc(place_ready, 1)

            def route_b(f, group):
                dve.wait_ge(exp_ready, NG * f + group + 1)
                v.tensor_tensor(kept[:], keep[:], expd[:], ALU.mult).then_inc(dve_own, 1)
                dve.wait_ge(place_ready, NG * f + group + 1)
                dve.wait_ge(dve_own, own.next())
                v.tensor_reduce(denom[:], kept[:], AX, ALU.add).then_inc(dve_own, 1)
                dve.wait_ge(dve_own, own.next())
                v.tensor_tensor(placed[:], place[:].unsqueeze(2).broadcast_to([P, TG, K, E]), onehot[:],
                                ALU.mult).then_inc(dve_own, 1)
                weight = xrow[:, :, TG * group:TG * (group + 1), C + 1].rearrange("p k t -> p t k")
                v.reciprocal(weight, denom[:])
                dve.wait_ge(dve_own, own.next())
                with nc.allow_low_precision(reason="one whole number of each eight is not zero"):
                    v.tensor_reduce(slot[:, group, :, :], placed[:], AX, ALU.add).then_inc(slot_ready, 1)

            def tables(f):
                dve.wait_ge(count_ready, f + 1)
                dve.wait_ge(consts_ready, 2)
                v.tensor_tensor(pad_tab[:, f, :], count_ps[0:1, :], region[0:1, :], ALU.add).then_inc(tables_ready, 1)
                v.tensor_tensor(over[:], thresholds[:], count_ps[0:1, :].unsqueeze(2).broadcast_to([1, E, NT]),
                                ALU.is_lt).then_inc(dve_own, 1)
                dve.wait_ge(dve_own, own.next())
                v.tensor_reduce(tiles_of[:], over[:], AX, ALU.add).then_inc(dve_own, 1)
                dve.wait_ge(dve_own, own.next())
                v.tensor_tensor_scan(tiles_end[:], ones_e[:], tiles_of[:], 0.0, ALU.mult, ALU.add).then_inc(dve_own, 1)
                dve.wait_ge(dve_own, own.next())
                v.tensor_tensor(past[:], tiles_end[:].unsqueeze(1).broadcast_to([1, NS, E]),
                                iota_s[:].unsqueeze(2).broadcast_to([1, NS, E]), ALU.is_le).then_inc(dve_own, 1)
                dve.wait_ge(dve_own, own.next())
                v.tensor_tensor(past_tiles[:], past[:], tiles_of[:].unsqueeze(1).broadcast_to([1, NS, E]), ALU.mult)
                v.tensor_reduce(expert_f[:], past[:], AX, ALU.add).then_inc(dve_own, 1)
                dve.wait_ge(dve_own, own.next())
                v.tensor_reduce(first_of[:], past_tiles[:], AX, ALU.add)
                v.scalar_tensor_tensor(row_a[:], expert_f[:], float(REG), iota_s128[:], ALU.mult, ALU.add)
                v.tensor_scalar(expert_tab[:, f, :], expert_f[:], float(E - 1), None, ALU.min).then_inc(dve_own, 1)
                dve.wait_ge(dve_own, own.next())
                v.scalar_tensor_tensor(row_tab[:, f, :], first_of[:], float(-P), row_a[:], ALU.mult,
                                       ALU.add).then_inc(tables_ready, 1)

            def experts(f):
                def x_lo(g, c):
                    s = c % RING
                    dve.wait_ge(xg_loaded[s], (g + (c // RING + 1 + f * uses(s))) * 16)
                    if isinstance(g, int):
                        sent = c // RING + f * uses(s)
                    else:
                        sent = g + (c // RING + f * uses(s))
                    if not (isinstance(sent, int) and sent == 0):
                        dve.wait_ge(y_scattered[s], sent * 16)
                    v.tensor_copy(result_row[:, s:s + 1], xg[:, s, C:C + 1])
                    v.tensor_copy(row_weight[:, s:s + 1], xg[:, s, C + 1:C + 2])
                    dve.wait_ge(xT_hi_ready, g * RING + (c + 1 + f * NS))
                    v.tensor_tensor(xT_lo[:, c % PR, :], xT_ps, xT_hi[:, c % PR, :].bitcast(F32),
                                    ALU.subtract).then_inc(xT_lo_ready, 1)

                def products(g, c):
                    dve.wait_ge(silu_ready, g * RING + (c + 1 + f * NS))
                    dve.wait_ge(up_ps_ready, g * RING + (c + 1 + f * NS))
                    v.tensor_tensor(h[:, c % PR, :], up_ps[c % PB][:], silu[:, c % PR, :], ALU.mult).then_inc(h_ready, 1)

                def step(g, c):
                    alone = isinstance(g, int)
                    if alone and c == 0:
                        x_lo(0, 0)
                        x_lo(0, 1)
                        products(0, 0)
                    if not alone or c + 2 < NS:
                        x_lo(g, c + 2)
                    if not alone or c + 1 < NS:
                        products(g, c + 1)
                    if not alone or c >= 1:
                        s = (c - 1) % RING
                        dve.wait_ge(y_ps_ready, g * RING + (c + f * NS))
                        v.tensor_scalar(y[:, s, :], y_ps, row_weight[:, s:s + 1], None, ALU.mult).then_inc(y_ready, 1)
                loop_tiles(dve, step)

            def combine(f, b, ready):
                s = slice(TPB * b, TPB * (b + 1))
                dve.wait_ge(y_loaded[b], 32 * (f + 1))
                v.tensor_tensor(Y[:, 0, s, :], Y[:, 0, s, :], Y[:, 1, s, :], ALU.add).then_inc(dve_own, 1)
                dve.wait_ge(dve_own, own.next())
                v.scalar_tensor_tensor(X[:, s, :], Y[:, 0, s, :], 0.5, X[:, s, :], ALU.mult, ALU.add).then_inc(ready, 1)

            dve.wait_ge(consts_ready, 1)
            tiles = [slice(TG * g, TG * (g + 1)) for g in range(NG)]
            for g in range(NG):
                dve.wait_ge(x_loaded[g], 16)
                stats_of(tiles[g], stats, mv, var_eps, var_ready)
                if g >= 1:
                    xn_rows(tiles[g - 1], g)
            copy_rows(tiles[0], 1)
            for g in range(NG):
                route_a(0, g)
                if g == 0:
                    xn_rows(tiles[NG - 1], NG)
                if g + 1 < NG:
                    copy_rows(tiles[g + 1], g + 2)
                route_b(0, g)
            tables(0)
            for e in range(E):
                dve.wait_ge(w13_hi_ready, e + 1)
                for i in range(2):
                    last = v.tensor_tensor(w13_lo[:, e, i, :], w13_raw[:, e, i, :], w13_hi[:, e, i, :].bitcast(F32),
                                           ALU.subtract)
                last.then_inc(w13_lo_ready, 1)
            experts(0)

            for s in range(STEPS):
                b = s - LAG_PLACE
                if 0 <= b < NB and b % BG == BG - 1:
                    route_b(1, b // BG)
                b = s - LAG_ROUTE
                if 0 <= b < NB and b % BG == BG - 1:
                    route_a(1, b // BG)
                b = s - LAG_X3
                if 0 <= b < NB:
                    t = slice(TPB * b, TPB * (b + 1))
                    dve.wait_ge(proj_ps_ready, b + 1)
                    v.tensor_tensor(X[:, t, :], proj_ps, X[:, t, :], ALU.add).then_inc(x3_ready, 1)
                    dve.wait_ge(x3_ready, b + 1)
                    stats_of(t, stats, mv, var_eps, var_ready)
                b = s - LAG_DIV
                if 0 <= b < NB:
                    i = b % 2
                    dve.wait_ge(att_ps_ready, b + 1)
                    v.tensor_scalar(den[:, i, :, :], att_ps[:, :, C:VW], EPS_ATTN, None, ALU.add).then_inc(dve_own, 1)
                    dve.wait_ge(dve_own, own.next())
                    v.reciprocal(rden[:, i, :, :], den[:, i, :, :]).then_inc(dve_own, 1)
                    dve.wait_ge(dve_own, own.next())
                    if b >= 2:
                        dve.wait_ge(attT_ps_ready, b - 1)
                    v.tensor_tensor(att[:, i, :, :].rearrange("p t (h d) -> p t h d", h=HEADS),
                                    att_ps[:, :, 0:C].rearrange("p t (h d) -> p t h d", h=HEADS),
                                    rden[:, i, :, :].unsqueeze(3).broadcast_to([P, TPB, HEADS, D]),
                                    ALU.mult).then_inc(att_ready, 1)
                b = s - LAG_KV
                if 0 <= b < NB:
                    dve.wait_ge(kvo_ps_ready, b + 1)
                    if b >= 2:
                        dve.wait_ge(att_ps_ready, b - 1)
                    v.tensor_tensor(kv[:, b % 2, :], kvo_ps, head_mask[:], ALU.mult).then_inc(kv_ready, 1)
                b = s
                if b < NB:
                    combine(0, b, x2_ready)
                    dve.wait_ge(x2_ready, b + 1)
                    stats_of(slice(TPB * b, TPB * (b + 1)), stats2, mv2, var_eps2, var2_ready)
                b = s - LAG_XN
                if 0 <= b < NB:
                    xn_rows(slice(TPB * b, TPB * (b + 1)), NG + b + 1)
                    copy_rows(slice(TPB * b, TPB * (b + 1)), NG + b + 1)
                b = s - LAG_XN2
                if 0 <= b < NB:
                    dve.wait_ge(rstd2_ready, b + 1)
                    if b >= 2:
                        dve.wait_ge(xn2T_ps_ready, b - 1)
                    normalise(lambda t: xn2[:, b % 2, t % TPB, :], slice(TPB * b, TPB * (b + 1)), mv2, rstd2, xn2_ready)
            tables(1)
            experts(1)
            for b in range(NB):
                combine(1, b, out_ready)

        @block.tensor
        def _(pe):
            mm = nc.tensor.matmul

            def xn_transposes(f, b):
                pe.wait_ge(xn_ready, NG + b + 1 if f else b // BG + 1)
                if NB * f + b:
                    pe.wait_ge(xnT_ready, NB * f + b)
                if f:
                    pe.wait_ge(xn2T_ready, min(b + LAG_XN_T - LAG_XN2_T, NB))
                for j in range(TPB):
                    last = nc.tensor.transpose(xnT_ps[:, j * P:(j + 1) * P], xrow[:, 0, TPB * b + j, 0:C], ident[:])
                last.then_inc(xnT_ps_ready, 1)

            def scores(f, b):
                pe.wait_ge(xnT_ready, NB * f + b + 1)
                done = NG * f + b // BG
                if done and b % BG == 0:
                    pe.wait_ge(S_ready, done)
                if done:
                    routed = done if b % BG == 1 else done - 1
                    if routed:
                        pe.wait_ge(place_ready, routed)
                for j in range(TPB):
                    last = mm(scores_ps[:, TPB * b + j, :], xnT[:, b % 2, j * P:(j + 1) * P], wgate_sb[:],
                              start=True, stop=True)
                last.then_inc(scores_ready, 1)

            def ranks(f, group):
                pe.wait_ge(chosen_ready, NG * f + group + 1)
                if group:
                    pe.wait_ge(carry_ready, (NG * f + group))
                mm(rank_ps, before[:], chosen[:], start=True, stop=False)
                for j in range(TG - 1):
                    mm(rank_ps[:, j + 1:TG, :], ones_b[:],
                       chosen[:, j:j + 1, :].broadcast_to([P, TG - 1 - j, E]), start=False, stop=False)
                mm(rank_ps, ones_b[:], carry[:, group:group + 1, :].broadcast_to([P, TG, E]),
                   start=False, stop=True).then_inc(rank_ready, 1)

            def counts(f):
                pe.wait_ge(carry_ready, NG * (f + 1))
                pe.wait_ge(place_ready, NG * (f + 1))
                mm(count_ps, ones_b[:], carry[:, NG, :], start=True, stop=True).then_inc(count_ready, 1)

            def experts(f):
                def expert_of(g, c):
                    return nc.tensor.value_load(expert_tab[0:1, f, bass.ds(g * RING + c, 1)], min_val=0, max_val=E - 1)

                def x_transpose(g, c):
                    s = c % RING
                    pe.wait_ge(xg_loaded[s], (g + (c // RING + 1 + f * uses(s))) * 16)
                    if not (isinstance(g, int) and c == 0 and f == 0):
                        pe.wait_ge(xT_lo_ready, g * RING + (c + f * NS))
                    nc.tensor.transpose(xT_ps, xg[:, s, 0:C], ident[:]).then_inc(xT_ps_ready, 1)

                def up(g, c):
                    s = c % PR
                    e = expert_of(g, c)
                    pe.wait_ge(xT_lo_ready, g * RING + (c + 1 + f * NS))
                    for i, (ps, ready) in enumerate(((gate_ps[c % PB], gate_ps_ready), (up_ps[c % PB], up_ps_ready))):
                        mm(ps[:], xT_hi[:, s, :], w13_hi[:, bass.ds(e, 1), i, :], start=True, stop=False)
                        mm(ps[:], xT_hi[:, s, :], w13_lo[:, bass.ds(e, 1), i, :], start=False, stop=False)
                        mm(ps[:], xT_lo[:, s, :], w13_hi[:, bass.ds(e, 1), i, :], start=False, stop=True)\
                            .then_inc(ready, 1)

                def down(g, c):
                    e = expert_of(g, c)
                    pe.wait_ge(hT_ready, g * RING + (c + 1 + f * NS))
                    if not (isinstance(g, int) and c == 0 and f == 0):
                        pe.wait_ge(y_ready, g * RING + (c + f * NS))
                    for j in range(FC):
                        last = mm(y_ps, hT[:, c % PR, j * P:(j + 1) * P], w2_sb[:, bass.ds(e, 1), j, :],
                                  start=(j == 0), stop=(j == FC - 1))
                    last.then_inc(y_ps_ready, 1)

                def step(g, c):
                    alone = isinstance(g, int)
                    if alone and c == 0:
                        x_transpose(0, 0)
                        x_transpose(0, 1)
                        up(0, 0)
                    if not alone or c + 2 < NS:
                        x_transpose(g, c + 2)
                    if not alone or c + 1 < NS:
                        up(g, c + 1)
                    if not alone or c >= 1:
                        down(g, c - 1)
                    if not alone or c < NS:
                        pe.wait_ge(h_ready, g * RING + (c + 1 + f * NS))
                        for j in range(FC):
                            last = nc.tensor.transpose(hT_ps[:, j * P:(j + 1) * P], h[:, c % PR, j * P:(j + 1) * P], ident[:])
                        last.then_inc(hT_ps_ready, 1)

                pe.wait_ge(tables_ready, 2 * f + 2)
                loop_tiles(pe, step)

            pe.wait_ge(consts_ready, 1)
            pe.wait_ge(wgate_loaded, 16)
            for b in range(NB):
                if b >= 3 and b % BG == 1:
                    ranks(0, b // BG - 1)
                xn_transposes(0, b)
                scores(0, b)
            ranks(0, NG - 1)
            counts(0)
            pe.wait_ge(w13_lo_ready, E)
            pe.wait_ge(w2_loaded, 16)
            experts(0)

            pe.wait_ge(wattn_loaded, 48)
            for s in range(STEPS):
                b = s - LAG_GATE
                if 0 <= b < NB:
                    scores(1, b)
                b = s - LAG_ROUTE
                if 0 <= b < NB and b % BG == BG - 1:
                    ranks(1, b // BG)
                b = s - LAG_XN_T
                if 0 <= b < NB:
                    xn_transposes(1, b)
                b = s - LAG_PROJ
                if 0 <= b < NB:
                    pe.wait_ge(attT_ready, b + 1)
                    if b:
                        pe.wait_ge(x3_ready, b)
                    for j in range(TPB):
                        mm(proj_ps[:, j, :], attT[:, b % 2, j * P:(j + 1) * P], wproj_sb[:], start=True, stop=False)
                        last = mm(proj_ps[:, j, :], ones_f[:], bproj_sb[:], start=False, stop=True)
                    last.then_inc(proj_ps_ready, 1)
                b = s - LAG_ATT_T
                if 0 <= b < NB:
                    pe.wait_ge(att_ready, b + 1)
                    if b:
                        pe.wait_ge(attT_ready, b)
                    for j in range(TPB):
                        last = nc.tensor.transpose(attT_ps[:, j * P:(j + 1) * P], att[:, b % 2, j, :], ident[:])
                    last.then_inc(attT_ps_ready, 1)
                b = s - LAG_ATT
                if 0 <= b < NB:
                    pe.wait_ge(q_ready, b + 1)
                    pe.wait_ge(kv_ready, b + 1)
                    if b:
                        pe.wait_ge(att_ready, b)
                    for j in range(TPB):
                        last = mm(att_ps[:, j, :], qT[:, b % QB, j * P:(j + 1) * P], kv[:, b % 2, :], start=True, stop=True)
                    last.then_inc(att_ps_ready, 1)
                b = s - LAG_KVO
                if 0 <= b < NB:
                    pe.wait_ge(kv_in_ready, b + 1)
                    if b:
                        pe.wait_ge(kv_ready, b)
                    for j in range(TPB):
                        last = mm(kvo_ps, kk[:, b % 2, j, :], vv[:, b % 2, j, :], start=(j == 0), stop=(j == TPB - 1))
                    last.then_inc(kvo_ps_ready, 1)
                b = s - LAG_QKV
                if 0 <= b < NB:
                    pe.wait_ge(xn2T_ready, b + 1)
                    if b:
                        pe.wait_ge(q_ready, b)
                        pe.wait_ge(kv_in_ready, b)
                    mm(q_ps, wqkv_sb[:, 0:C], xn2T[:, b % 2, :], start=True, stop=True).then_inc(q_ps_ready, 1)
                    for j in range(TPB):
                        last = mm(kv_ps[:, j, :], xn2T[:, b % 2, j * P:(j + 1) * P], wqkv_sb[:, C:3 * C],
                                  start=True, stop=True)
                    last.then_inc(kv_ps_ready, 1)
                b = s - LAG_XN2_T
                if 0 <= b < NB:
                    pe.wait_ge(xn2_ready, b + 1)
                    if b:
                        pe.wait_ge(xn2T_ready, b)
                    for j in range(TPB):
                        last = nc.tensor.transpose(xn2T_ps[:, j * P:(j + 1) * P], xn2[:, b % 2, j, :], ident[:])
                    last.then_inc(xn2T_ps_ready, 1)
            counts(1)
            experts(1)


def kernel(L0_attn_x, L0_attn_W_qkv, L0_attn_W_proj, L0_attn_b_proj, L0_ffn_gate_w, L0_ffn_w1, L0_ffn_w2, L0_ffn_w3):
    import numpy as np
    import concourse.bacc as bacc
    from concourse.bass_utils import run_bass_kernel_spmd

    def laid(a):
        return np.ascontiguousarray(a)

    inputs = {
        "x": laid(np.asarray(L0_attn_x).reshape(NT, P, C).transpose(1, 0, 2)),
        "w_qkv": laid(np.asarray(L0_attn_W_qkv).T),
        "w_proj": laid(np.asarray(L0_attn_W_proj).T),
        "b_proj": laid(np.asarray(L0_attn_b_proj).reshape(1, C)),
        "w_gate": laid(np.asarray(L0_ffn_gate_w).T),
        "w1": laid(np.asarray(L0_ffn_w1).transpose(2, 0, 1)),
        "w3": laid(np.asarray(L0_ffn_w3).transpose(2, 0, 1)),
        "w2": laid(np.asarray(L0_ffn_w2).transpose(2, 0, 1).reshape(FC, P, E, C).transpose(1, 2, 0, 3)),
    }
    nc = bacc.Bacc("TRN2", target_bir_lowering=False, num_devices=1)
    args = [nc.dram_tensor(f"{name}_in", a.shape, F32, kind="ExternalInput").ap() for name, a in inputs.items()]
    out = nc.dram_tensor("out", (P, NT, C), F32, kind="ExternalOutput").ap()
    build(nc, *args, out)
    r = run_bass_kernel_spmd(nc, [{f"{name}_in": a for name, a in inputs.items()}], core_ids=[0])
    return np.ascontiguousarray(r.results[0]["out"].transpose(1, 0, 2)).reshape(NB, TB, C)
```

```python
from contextlib import ExitStack

import concourse.bass as bass
from concourse import mybir

F32 = mybir.dt.float32
F32R = mybir.dt.float32r
BF16 = mybir.dt.bfloat16
I32 = mybir.dt.int32
U32 = mybir.dt.uint32
ALU = mybir.AluOpType
ACT = mybir.ActivationFunctionType
AX = mybir.AxisListType.X

P = 128
C = 128
T = 2048
NT = T // P
NB = 8
TPB = NT // NB
TB = TPB * P
E = 8
F = 512
FC = F // P
K = 2
NL = 4
TL = NT // NL
BL = NB // NL
GROUPS = ((2, 2, 2, 2), (1, 1, 1, 1, 2, 2))
TG = max(GROUPS[0] + GROUPS[1]) * TPB
NS = (K * T + E * (P - 1)) // P
REG = T + P
SPARE = NS - K * T // P
XROWS = E * REG + SPARE * P
YROWS = K * T + (E + SPARE) * P
ROW = C + 2
HEADS = 4
D = C // HEADS
VW = C + HEADS
RING = 6
PR = 3
PB = 2
LOOPS = (NS - 3) // RING
ALWAYS = LOOPS * RING
assert NS == 39 and LOOPS * RING == NS - 3
HALF = NB // 2
EARLY = -(-(HALF * TB * K - E * (P - 1)) // P)
LATE_AT = 0
HEAD = 2 * RING
assert EARLY == 9 and RING < EARLY < HEAD and NB == E
EPS_LN = 1e-5
EPS_ATTN = 1e-15
JITTER = 0.02


class Count:

    def __init__(self):
        self.n = 0

    def next(self):
        self.n += 1
        return self.n


def build(nc, x, w_qkv, w_proj, b_proj, w_gate, w1, w3, w2, out):
    with ExitStack() as ctx:
        def sb(name, shape, dt=F32):
            return ctx.enter_context(nc.sbuf_tensor(name, shape, dt))

        def sem(name):
            return ctx.enter_context(nc.semaphore(name))

        sorted_rows = [nc.dram_tensor(f"sorted_rows{f}", [XROWS, ROW], F32, kind="Internal").ap() for f in range(2)]
        results = [nc.dram_tensor(f"results{f}", [YROWS, C], F32, kind="Internal").ap() for f in range(2)]
        results_tk = [r[0:K * T, :].rearrange("(t k p) c -> p t k c", k=K, p=P) for r in results]

        w13_raw = sb("w13_raw", [P, E, 2, F])
        w13_hi = sb("w13_hi", [P, E, 2, F], F32R)
        w13_lo = sb("w13_lo", [P, E, 2, F], F32R)
        w2_sb = sb("w2_sb", [P, E, FC, C])
        wqkv_sb = sb("wqkv_sb", [C, 3 * C])
        wproj_sb = sb("wproj_sb", [C, C])
        bproj_sb = sb("bproj_sb", [1, C])
        wgate_sb = sb("wgate_sb", [C, E])

        ident = sb("ident", [P, P])
        ones_f = sb("ones_f", [1, P])
        before = sb("before", [P, P], BF16)
        ones_b = sb("ones_b", [P, P], BF16)
        head_mask = sb("head_mask", [P, VW])
        iota_e = sb("iota_e", [P, E], I32)
        region = sb("region", [P, E], I32)
        thresholds = sb("thresholds", [1, E, NT], I32)
        iota_s = sb("iota_s", [1, NS], I32)
        iota_s128 = sb("iota_s128", [1, NS], I32)
        ones_e = sb("ones_e", [1, E])
        minus_half = sb("minus_half", [P, TL])
        pad_rows = sb("pad_rows", [P, E + SPARE, ROW])

        X = sb("X", [P, NT, C])
        Y = w13_raw[:, 0:E // 2, :, :].rearrange("p e i f -> p (e i f)").rearrange("p (t k c) -> p t k c", k=K, c=C)
        xrow = sb("xrow", [P, K, NT, ROW])
        stats = sb("stats", [P, NT, 6])
        mv = sb("mv", [P, NT, 2])
        var_eps = sb("var_eps", [P, NT])
        rstd = sb("rstd", [P, NT])
        shift = sb("shift", [P, NT])
        stats2 = sb("stats2", [P, NT, 6])
        mv2 = sb("mv2", [P, NT, 2])
        var_eps2 = sb("var_eps2", [P, NT])
        rstd2 = sb("rstd2", [P, NT])
        shift2 = sb("shift2", [P, NT])
        xnT = sb("xnT", [C, 2, TB])
        S = sb("S", [P, TG, E])
        Sabs = sb("Sabs", [P, TG, E])
        top = sb("top", [P, TG, 8])
        top_at = sb("top_at", [P, TG, 8], U32)
        gap = sb("gap", [P, TG, K, E])
        gap0 = sb("gap0", [P, TG, K, E])
        factor = sb("factor", [P, TG, K, E])
        keep = sb("keep", [P, TG, K, E])
        onehot = sb("onehot", [P, TG, K, E])
        expd = sb("expd", [P, TG, K, E])
        kept = sb("kept", [P, TG, K, E])
        denom = sb("denom", [P, TG, K])
        chosen = sb("chosen", [P, TG, E], BF16)
        chosen_sum = sb("chosen_sum", [P, E])
        carry = sb("carry", [P, NB + 1, E], BF16)
        place = sb("place", [P, TG, E])
        placed = sb("placed", [P, TG, K, E])
        slot = sb("slot", [P, NT, K], I32)

        count = sb("count", [1, E])
        over = sb("over", [1, E, NT])
        tiles_of = sb("tiles_of", [1, E])
        tiles_end = sb("tiles_end", [1, E])
        early_end = sb("early_end", [1, E])
        early_of = sb("early_of", [1, E + 1])
        early_step = sb("early_step", [1, E])
        late_start = sb("late_start", [1, NS])
        skipped = sb("skipped", [1, E])
        past = sb("past", [1, NS, E])
        past_tiles = sb("past_tiles", [1, NS, E])
        expert_f = sb("expert_f", [1, NS])
        first_of = sb("first_of", [1, NS])
        row_a = sb("row_a", [1, NS])
        expert_tab = sb("expert_tab", [1, 2, NS], I32)
        row_tab = sb("row_tab", [1, 2, NS], I32)
        pad_tab = sb("pad_tab", [1, 2, E], I32)
        used_tab = sb("used_tab", [1, 2], I32)

        xg = sb("xg", [P, RING, ROW])
        result_row = sb("result_row", [P, RING], I32)
        row_weight = sb("row_weight", [P, RING])
        xT_hi = sb("xT_hi", [C, PR, P], F32R)
        xT_lo = sb("xT_lo", [C, PR, P], F32R)
        silu = sb("silu", [P, PR, F])
        h = sb("h", [P, PR, F])
        hT = sb("hT", [P, PR, F])
        y = sb("y", [P, RING, C])

        xn2 = sb("xn2", [P, 2, TPB, C])
        xn2T = sb("xn2T", [C, 2, TB])
        qT = sb("qT", [C, 2, TB])
        kk = sb("kk", [P, 2, TPB, C])
        vv = sb("vv", [P, 2, TPB, VW])
        kv = sb("kv", [C, 2, VW])
        den = sb("den", [P, 2, TPB, HEADS])
        rden = sb("rden", [P, 2, TPB, HEADS])
        att = sb("att", [P, 2, TPB, C])
        attT = sb("attT", [C, 2, TB])

        banks = [ctx.enter_context(nc.psum_tensor(f"bank{i}", [P, 512], F32)) for i in range(8)]
        gate_ps = banks[0:PB]
        up_ps = banks[PB:2 * PB]
        hT_ps = banks[4]
        y_ps = banks[5][:, 0:C]
        xT_ps = banks[6][:, 0:P]
        xn2T_ps = banks[0][:, 0:TB]
        xnT_ps = banks[0][:, TB:2 * TB]
        q_ps = banks[1][:, 0:TB]
        kv_ps = banks[2][:, :].rearrange("p (t c) -> p t c", t=TPB)
        kvo_ps = banks[3][:, 0:VW]
        att_ps = banks[4][:, 0:TPB * VW].rearrange("p (t c) -> p t c", t=TPB)
        attT_ps = banks[5][:, 0:TB]
        proj_ps = banks[6][:, 0:TB].rearrange("p (t c) -> p t c", t=TPB)
        scores_ps = banks[7][:, 0:NT * E].rearrange("p (t e) -> p t e", t=NT)
        rank_ps = banks[7][:, NT * E:NT * E + TG * E].rearrange("p (t e) -> p t e", t=TG)
        count_ps = banks[7][:, 256:256 + E]

        x_loaded = [sem(f"x_loaded{g}") for g in range(NL)]
        wgate_loaded = sem("wgate_loaded")
        w13_loaded = [sem(f"w13_loaded{e}") for e in range(E)]
        w2_loaded = sem("w2_loaded")
        wattn_loaded = sem("wattn_loaded")
        y_loaded = [sem(f"y_loaded{b}") for b in range(NB)]
        consts_ready = sem("consts_ready")
        pool_own = sem("pool_own")
        dve_own = sem("dve_own")
        w13_hi_ready = sem("w13_hi_ready")
        w13_lo_ready = sem("w13_lo_ready")
        var_ready = sem("var_ready")
        rstd_ready = sem("rstd_ready")
        shift_ready = sem("shift_ready")
        xn_ready = sem("xn_ready")
        xnT_ps_ready = sem("xnT_ps_ready")
        xnT_ready = sem("xnT_ready")
        scores_ready = sem("scores_ready")
        S_ready = sem("S_ready")
        gap_ready = sem("gap_ready")
        exp_ready = sem("exp_ready")
        chosen_ready = sem("chosen_ready")
        rank_ready = sem("rank_ready")
        place_ready = sem("place_ready")
        slot_ready = sem("slot_ready")
        carry_ready = sem("carry_ready")
        count_ready = sem("count_ready")
        count_copied = sem("count_copied")
        tables_ready = sem("tables_ready")
        rows_scattered = [[sem(f"rows_scattered{f}_{half}") for half in range(2)] for f in range(2)]
        pads_written = sem("pads_written")
        xg_loaded = [[sem(f"xg_loaded{f}_{i}") for i in range(RING)] for f in range(2)]
        xT_ps_ready = [sem(f"xT_ps_ready{f}") for f in range(2)]
        xT_hi_ready = [sem(f"xT_hi_ready{f}") for f in range(2)]
        xT_lo_ready = [sem(f"xT_lo_ready{f}") for f in range(2)]
        gate_ps_ready = [sem(f"gate_ps_ready{f}") for f in range(2)]
        up_ps_ready = [sem(f"up_ps_ready{f}") for f in range(2)]
        silu_ready = [sem(f"silu_ready{f}") for f in range(2)]
        h_ready = [sem(f"h_ready{f}") for f in range(2)]
        hT_ps_ready = [sem(f"hT_ps_ready{f}") for f in range(2)]
        hT_ready = [sem(f"hT_ready{f}") for f in range(2)]
        y_ps_ready = [sem(f"y_ps_ready{f}") for f in range(2)]
        y_ready = [sem(f"y_ready{f}") for f in range(2)]
        y_scattered = [[sem(f"y_scattered{f}_{i}") for i in range(RING)] for f in range(2)]
        x2_ready = sem("x2_ready")
        var2_ready = sem("var2_ready")
        rstd2_ready = sem("rstd2_ready")
        shift2_ready = sem("shift2_ready")
        xn2_ready = sem("xn2_ready")
        xn2T_ps_ready = sem("xn2T_ps_ready")
        xn2T_ready = sem("xn2T_ready")
        q_ps_ready = sem("q_ps_ready")
        kv_ps_ready = sem("kv_ps_ready")
        q_ready = sem("q_ready")
        kv_in_ready = sem("kv_in_ready")
        kvo_ps_ready = sem("kvo_ps_ready")
        kv_ready = sem("kv_ready")
        att_ps_ready = sem("att_ps_ready")
        att_ready = sem("att_ready")
        attT_ps_ready = sem("attT_ps_ready")
        attT_ready = sem("attT_ready")
        proj_ps_ready = sem("proj_ps_ready")
        x3_ready = sem("x3_ready")
        y_sum_ready = sem("y_sum_ready")
        stats_ready = sem("stats_ready")
        mean_ready = sem("mean_ready")
        stats2_ready = sem("stats2_ready")
        mean2_ready = sem("mean2_ready")
        den_ready = sem("den_ready")
        rden_ready = sem("rden_ready")
        out_stored = sem("out_stored")

        block = ctx.enter_context(nc.Block())

        def group_of(b, f):
            ends = [sum(GROUPS[f][:i + 1]) for i in range(len(GROUPS[f]))]
            i = sum(end <= b for end in ends)
            return len(GROUPS[0]) * f + i + 1, range(ends[i] - GROUPS[f][i], ends[i])

        def group_done(b, f, late=True):
            group, batches = group_of(b, f)
            if b < batches.stop - 1 or b == NB - 1 and not late:
                return 0, 0
            return group, len(batches) * TPB

        def pipeline(*stages):
            for s in range(NB + max(lag for _, lag in stages)):
                for stage, lag in stages:
                    if 0 <= s - lag < NB:
                        stage(s - lag)

        def loop_tiles(engine, f, step):
            for c in range(HEAD + 1):
                step(0, c)
            engine.wait_ge(tables_ready, 3 * f + 3)
            used = engine.value_load(used_tab[0:1, f:f + 1], min_val=0, max_val=NS)
            with engine.Fori(HEAD // RING, LOOPS) as g:
                for c in range(1, RING + 1):
                    step(g, c)
            for c in range(ALWAYS + 1, NS + 1):
                with engine.If(used > c - 1):
                    step(0, c)

        @block.sync
        def _(sp):
            for g in range(NL):
                sp.dma_start(X[:, TL * g:TL * g + TL, :], x[:, TL * g:TL * g + TL, :]).then_inc(x_loaded[g], 16)
                if g == 0:
                    sp.dma_start(wgate_sb[:], w_gate).then_inc(wgate_loaded, 16)
            for e in range(E):
                sp.dma_start(w13_raw[:, e, 0, :], w1[:, e, :]).then_inc(w13_loaded[e], 16)
                sp.dma_start(w13_raw[:, e, 1, :], w3[:, e, :]).then_inc(w13_loaded[e], 16)
            sp.dma_start(w2_sb[:], w2).then_inc(w2_loaded, 16)
            sp.dma_start(wqkv_sb[:], w_qkv).then_inc(wattn_loaded, 16)
            sp.dma_start(wproj_sb[:], w_proj).then_inc(wattn_loaded, 16)
            sp.dma_start(bproj_sb[:], b_proj).then_inc(wattn_loaded, 16)
            sp.wait_ge(consts_ready, 2)
            for f in range(2):
                sp.dma_start(sorted_rows[f][E * REG:XROWS, :].rearrange("(n p) r -> p n r", p=P),
                             pad_rows[:, E:E + SPARE, :]).then_inc(pads_written, 16)

            for f in range(2):
                def load_tile(g, c, f=f):
                    s = c % RING
                    if not (isinstance(g, int) and c < RING):
                        sp.wait_ge(xT_lo_ready[f], g * RING + (c - RING + 1))
                    at = nc.sync.value_load(row_tab[0:1, f, bass.ds(g * RING + c, 1)], min_val=0, max_val=XROWS - P)
                    sp.dma_start(xg[:, s, :], sorted_rows[f][bass.ds(at, P), :]).then_inc(xg_loaded[f][s], 16)

                sp.wait_ge(tables_ready, 3 * f + 1)
                sp.wait_ge(rows_scattered[f][0], 16 * K * TPB * HALF)
                for c in range(EARLY):
                    load_tile(0, c)
                sp.wait_ge(tables_ready, 3 * f + 2)
                for e in range(E):
                    first = nc.sync.value_load(pad_tab[0:1, f, e:e + 1], min_val=0, max_val=E * REG - P)
                    sp.dma_start(sorted_rows[f][bass.ds(first, P), :], pad_rows[:, e, :]).then_inc(pads_written, 16)
                sp.wait_ge(tables_ready, 3 * f + 3)
                sp.wait_ge(rows_scattered[f][1], 16 * K * TPB * (NB - HALF))
                sp.wait_ge(pads_written, 16 * (2 + E * (f + 1)))
                for c in range(EARLY, HEAD):
                    load_tile(0, c)
                with sp.Fori(HEAD // RING - 1, LOOPS - 1) as g:
                    for c in range(RING, 2 * RING):
                        load_tile(g, c)
                for c in range(LOOPS * RING, NS):
                    load_tile(0, c)

                for s in range(RING):
                    sp.wait_ge(y_scattered[f][s], 16 * LOOPS)
                used = nc.sync.value_load(used_tab[0:1, f:f + 1], min_val=0, max_val=NS)
                for i in range(ALWAYS, NS):
                    with sp.If(used > i):
                        sp.wait_ge(y_scattered[f][i % RING], 16 * (i // RING + 1))
                for b in range(NB):
                    sp.dma_start(Y[:, TPB * b:TPB * (b + 1), :, :],
                                 results_tk[f][:, TPB * b:TPB * (b + 1), :, :]).then_inc(y_loaded[b], 16)
            for b in range(NB):
                sp.wait_ge(x2_ready, NB + b + 1)
                sp.dma_start(out[:, TPB * b:TPB * (b + 1), :], X[:, TPB * b:TPB * (b + 1), :]).then_inc(out_stored, 16)
            sp.wait_ge(out_stored, 16 * NB)

        @block.gpsimd
        def _(pool):
            own = Count()
            g = nc.gpsimd
            g.memset(minus_half[:], -0.5)
            g.memset(ident[:], 0.0).then_inc(pool_own, 1)
            pool.wait_ge(pool_own, own.next())
            g.affine_select(out=ident[:], in_=ident[:], compare_op=ALU.not_equal, fill=1.0, base=0,
                            pattern=[[-1, P]], channel_multiplier=1)
            g.memset(before[:], 1.0)
            g.memset(ones_b[:], 1.0)
            g.iota(iota_e[:], [[1, E]], base=0, channel_multiplier=0)
            g.iota(region[:], [[REG, E]], base=0, channel_multiplier=0)
            g.memset(carry[:, 0, :], 0.0)
            for k in range(K):
                g.iota(xrow[:, k, :, C:C + 1], [[K * P, NT], [0, 1]], base=k * P, channel_multiplier=1,
                       allow_small_or_imprecise_dtypes=True)
            g.memset(ones_f[:], 1.0).then_inc(pool_own, 1)
            pool.wait_ge(pool_own, own.next())
            g.affine_select(out=before[:], in_=before[:], compare_op=ALU.is_gt, fill=0.0, base=0,
                            pattern=[[1, P]], channel_multiplier=-1).then_inc(consts_ready, 1)

            def rstd_of(s, v, r, out_sem):
                g.tensor_tensor(r[:, s], v[:, s], minus_half[:, 0:s.stop - s.start], ALU.pow).then_inc(out_sem, 1)

            def scatter(f, b, j):
                pool.wait_ge(slot_ready, group_of(b, f)[0])
                for k in range(K):
                    at = slot[:, TPB * b + j, k:k + 1]
                    g.indirect_dma_start(
                        out=sorted_rows[f], out_offset=bass.IndirectOffsetOnAxis(ap=at, axis=0),
                        in_=xrow[:, k, TPB * b + j, :], in_offset=None).then_inc(rows_scattered[f][b // HALF], 16)

            def send_results(f):
                def send(i):
                    s = i % RING
                    pool.wait_ge(y_ready[f], i + 1)
                    g.indirect_dma_start(
                        out=results[f], out_offset=bass.IndirectOffsetOnAxis(ap=result_row[:, s:s + 1], axis=0),
                        in_=y[:, s, :], in_offset=None).then_inc(y_scattered[f][s], 16)

                for b in group_of(NB - 1, f)[1]:
                    for j in range(TPB):
                        scatter(f, b, j)
                    if b < NB - 1:
                        send(0)
                for i in range(1, ALWAYS):
                    send(i)
                pool.wait_ge(tables_ready, 3 * f + 3)
                used = g.value_load(used_tab[0:1, f:f + 1], min_val=0, max_val=NS)
                for i in range(ALWAYS, NS):
                    with pool.If(used > i):
                        send(i)

            def batch_rstd(b):
                pool.wait_ge(var_ready, NL + b + 1)
                rstd_of(slice(TPB * b, TPB * (b + 1)), var_eps, rstd, rstd_ready)

            def batch_rstd2(b):
                pool.wait_ge(var2_ready, b + 1)
                rstd_of(slice(TPB * b, TPB * (b + 1)), var_eps2, rstd2, rstd2_ready)

            for n in range(NL):
                pool.wait_ge(var_ready, n + 1)
                rstd_of(slice(TL * n, TL * (n + 1)), var_eps, rstd, rstd_ready)
            g.memset(head_mask[:], 1.0)
            g.memset(pad_rows[:], 0.0)
            g.iota(thresholds[:], [[0, E], [P, NT]], base=0, channel_multiplier=0)
            g.iota(iota_s[:], [[1, NS]], base=0, channel_multiplier=0)
            g.iota(iota_s128[:], [[P, NS]], base=0, channel_multiplier=0)
            g.memset(ones_e[:], 1.0)
            g.memset(vv[:, :, :, C:VW], 1.0).then_inc(pool_own, 1)
            pool.wait_ge(pool_own, own.next())
            g.iota(pad_rows[:, :, C:C + 1], [[P, E + SPARE], [0, 1]], base=K * T, channel_multiplier=1,
                   allow_small_or_imprecise_dtypes=True)
            blocks = head_mask[:, 0:C].rearrange("p (h d) -> p h d", h=HEADS)
            g.affine_select(out=blocks, in_=blocks, compare_op=ALU.is_ge, fill=0.0, base=0,
                            pattern=[[-D, HEADS], [0, D]], channel_multiplier=1)
            heads = head_mask[:, C:VW]
            g.affine_select(out=heads, in_=heads, compare_op=ALU.is_ge, fill=0.0, base=0,
                            pattern=[[-D, HEADS]], channel_multiplier=1).then_inc(pool_own, 1)
            pool.wait_ge(pool_own, own.next())
            g.affine_select(out=blocks, in_=blocks, compare_op=ALU.is_ge, fill=0.0, base=D - 1,
                            pattern=[[D, HEADS], [0, D]], channel_multiplier=-1)
            g.affine_select(out=heads, in_=heads, compare_op=ALU.is_ge, fill=0.0, base=D - 1,
                             pattern=[[D, HEADS]], channel_multiplier=-1).then_inc(consts_ready, 1)
            for b in range(NB - GROUPS[0][-1]):
                for j in range(TPB):
                    scatter(0, b, j)
            send_results(0)
            def scatter_tile(b, j):
                if b < NB - GROUPS[1][-1]:
                    scatter(1, b, j)

            pipeline(
                (batch_rstd2, 0), (lambda b: scatter_tile(b, 0), 8), (lambda b: scatter_tile(b, 1), 8),
                (batch_rstd, 4)
            )
            send_results(1)

        @block.scalar
        def _(act):
            def copy(out, in_, func=ACT.Copy):
                return nc.scalar.activation(out, in_, func)

            def normalise(out, b, r, sh, ready):
                for j in range(TPB):
                    t = TPB * b + j
                    last = nc.scalar.activation(out[:, j, :], X[:, t, :], ACT.Identity, bias=sh[:, t:t + 1],
                                                scale=r[:, t:t + 1])
                last.then_inc(ready, 1)

            def xn(b, f=1):
                act.wait_ge(shift_ready, NL + b + 1 if f else b // BL + 1)
                normalise(xrow[:, 0, TPB * b:TPB * (b + 1), 0:C], b, rstd, shift, xn_ready)

            def xnT_copy(b, f=1):
                act.wait_ge(xnT_ps_ready, NB * f + b + 1)
                if b >= 2:
                    act.wait_ge(scores_ready, NB * f + b - 1)
                copy(xnT[:, b % 2, :], xnT_ps).then_inc(xnT_ready, 1)

            def scores_copy(b, f=1):
                group, n = group_done(b, f)
                if group:
                    act.wait_ge(scores_ready, NB * f + b + 1)
                    if group > 1:
                        act.wait_ge(gap_ready, group - 1)
                    part = scores_ps[:, TPB * (b + 1) - n:TPB * (b + 1), :]
                    copy(S[:, 0:n, :], part)
                    copy(Sabs[:, 0:n, :], part, ACT.Abs).then_inc(S_ready, 1)

            def routing_exp(b, f=1, late=False):
                group, n = group_done(b, f, late)
                if group:
                    act.wait_ge(gap_ready, group)
                    copy(expd[:, 0:n], gap0[:, 0:n], ACT.Exp).then_inc(exp_ready, 1)

            def experts(f):
                def x_hi(g, c):
                    act.wait_ge(xT_ps_ready[f], g * RING + (c + 1))
                    copy(xT_hi[:, c % PR, :], xT_ps).then_inc(xT_hi_ready[f], 1)

                def silus(g, c):
                    act.wait_ge(gate_ps_ready[f], g * RING + (c + 1))
                    copy(silu[:, c % PR, :], gate_ps[c % PB][:], ACT.Silu).then_inc(silu_ready[f], 1)

                def step(g, c):
                    alone = isinstance(g, int)
                    if alone and c == 0:
                        x_hi(0, 0)
                        x_hi(0, 1)
                        routing_exp(NB - 1, f, late=True)
                        silus(0, 0)
                    if not alone or c + 2 < NS:
                        x_hi(g, c + 2)
                    if not alone or c + 1 < NS:
                        silus(g, c + 1)
                    if not alone or c < NS:
                        act.wait_ge(hT_ps_ready[f], g * RING + (c + 1))
                        copy(hT[:, c % PR, :], hT_ps[:]).then_inc(hT_ready[f], 1)
                loop_tiles(act, f, step)

            def w13_upper(e):
                act.wait_ge(w13_loaded[e], 32)
                copy(w13_hi[:, e, 0, :], w13_raw[:, e, 0, :])
                copy(w13_hi[:, e, 1, :], w13_raw[:, e, 1, :]).then_inc(w13_hi_ready, 1)

            pipeline(
                (lambda b: xn(b, 0), 0), (lambda b: xnT_copy(b, 0), 1), (w13_upper, 5),
                (lambda b: scores_copy(b, 0), 1), (lambda b: routing_exp(b, 0), 2)
            )
            experts(0)

            def xn2_rows(b):
                act.wait_ge(shift2_ready, b + 1)
                if b >= 2:
                    act.wait_ge(xn2T_ps_ready, b - 1)
                normalise(xn2[:, b % 2, :, :], b, rstd2, shift2, xn2_ready)

            def xn2T_copy(b):
                act.wait_ge(xn2T_ps_ready, b + 1)
                if b >= 2:
                    act.wait_ge(q_ps_ready, b - 1)
                copy(xn2T[:, b % 2, :], xn2T_ps).then_inc(xn2T_ready, 1)

            def kv_copy(b):
                act.wait_ge(kv_ps_ready, b + 1)
                if b >= 2:
                    act.wait_ge(kvo_ps_ready, b - 1)
                copy(kk[:, b % 2, :, :], kv_ps[:, :, 0:C], ACT.Relu)
                copy(vv[:, b % 2, :, 0:C], kv_ps[:, :, C:2 * C]).then_inc(kv_in_ready, 1)

            def q_copy(b):
                act.wait_ge(q_ps_ready, b + 1)
                if b >= 2:
                    act.wait_ge(att_ps_ready, b - 1)
                copy(qT[:, b % 2, :], q_ps, ACT.Relu).then_inc(q_ready, 1)

            def attT_copy(b):
                act.wait_ge(attT_ps_ready, b + 1)
                if b >= 2:
                    act.wait_ge(proj_ps_ready, b - 1)
                copy(attT[:, b % 2, :], attT_ps).then_inc(attT_ready, 1)

            pipeline(
                (xn2_rows, 0), (xnT_copy, 5), (kv_copy, 1), (scores_copy, 5), (attT_copy, 2),
                (xn2T_copy, 0), (q_copy, 1), (xn, 4), (routing_exp, 5)
            )
            experts(1)

        @block.vector
        def _(dve):
            own = Count()
            v = nc.vector

            def stats_of(s, st, m, ve, ready):
                for t in range(s.start, s.stop):
                    last = v.bn_stats(st[:, t, :], X[:, t, :])
                last.then_inc(dve_own, 1)
                dve.wait_ge(dve_own, own.next())
                for t in range(s.start, s.stop):
                    last = v.bn_aggr(m[:, t, :], st[:, t, :])
                last.then_inc(dve_own, 1)
                dve.wait_ge(dve_own, own.next())
                v.tensor_scalar(ve[:, s], m[:, s, 1], EPS_LN, None, ALU.add).then_inc(ready, 1)

            def shift_of(s, m, r, sh, ready):
                v.scalar_tensor_tensor(sh[:, s], m[:, s, 0], -1.0, r[:, s], ALU.mult, ALU.mult).then_inc(ready, 1)

            def copy_rows(b, f=1):
                s = slice(TPB * b, TPB * (b + 1))
                dve.wait_ge(xn_ready, NB * f + b + 1)
                v.tensor_copy(xrow[:, 1, s, 0:C], xrow[:, 0, s, 0:C])

            reached = {}

            def route_top(b, f=1, late=False):
                group, n = group_done(b, f, late)
                if not group:
                    return
                dve.wait_ge(S_ready, group)
                for t in range(n):
                    last = v.max(top[:, t, :], S[:, t, :])
                last.then_inc(dve_own, 1)
                dve.wait_ge(dve_own, own.next())
                best = top[:, 0:n, 0:K].unsqueeze(3).broadcast_to([P, n, K, E])
                v.tensor_tensor(gap[:, 0:n], S[:, 0:n].unsqueeze(2).broadcast_to([P, n, K, E]), best, ALU.subtract)
                v.tensor_tensor(factor[:, 0:n], Sabs[:, 0:n].unsqueeze(2).broadcast_to([P, n, K, E]), best, ALU.max)
                for t in range(n):
                    last = v.max_index(top_at[:, t, :], top[:, t, :], S[:, t, :])
                last.then_inc(dve_own, 1)
                reached["top"] = own.next()

            def route_choose(b, f=1, late=False):
                group, n = group_done(b, f, late)
                if not group:
                    return
                dve.wait_ge(dve_own, reached["top"])
                v.tensor_scalar(gap0[:, 0:n], gap[:, 0:n], 0.0, None, ALU.min).then_inc(gap_ready, 1)
                v.tensor_tensor(onehot[:, 0:n], top_at[:, 0:n, 0:K].unsqueeze(3).broadcast_to([P, n, K, E]),
                                iota_e[:].unsqueeze(1).unsqueeze(1).broadcast_to([P, n, K, E]),
                                ALU.is_equal).then_inc(dve_own, 1)
                dve.wait_ge(dve_own, own.next())
                if group > 1:
                    dve.wait_ge(rank_ready, group - 1)
                v.tensor_tensor(chosen[:, 0:n], onehot[:, 0:n, 0, :], onehot[:, 0:n, 1, :], ALU.add)\
                    .then_inc(chosen_ready, 1)
                v.scalar_tensor_tensor(keep[:, 0:n], factor[:, 0:n], -JITTER, gap[:, 0:n], ALU.mult, ALU.is_le)\
                    .then_inc(dve_own, 1)
                reached["keep"] = own.next()

            def route_count(b, f=1, late=False):
                group, n = group_done(b, f, late)
                if not group:
                    return
                dve.wait_ge(dve_own, reached["keep"])
                v.tensor_tensor(keep[:, 0:n, 1, :], keep[:, 0:n, 1, :], onehot[:, 0:n, 0, :], ALU.is_gt)
                v.tensor_reduce(chosen_sum[:], chosen[:, 0:n].rearrange("p t e -> p e t"), AX, ALU.add)\
                    .then_inc(dve_own, 1)
                dve.wait_ge(dve_own, own.next())
                v.tensor_tensor(carry[:, b + 1, :], carry[:, b + 1 - n // TPB, :], chosen_sum[:], ALU.add)\
                    .then_inc(carry_ready, 1)

            def place_rows(b, f=1, late=False):
                group, n = group_done(b, f, late)
                if not group:
                    return
                dve.wait_ge(rank_ready, group)
                v.tensor_tensor(place[:, 0:n], rank_ps[:, 0:n, :], region[:].unsqueeze(1).broadcast_to([P, n, E]),
                                ALU.add).then_inc(place_ready, 1)
                dve.wait_ge(exp_ready, group)
                v.tensor_tensor(kept[:, 0:n], keep[:, 0:n], expd[:, 0:n], ALU.mult).then_inc(dve_own, 1)
                reached["kept"] = own.next()

            def place_sums(b, f=1, late=False):
                group, n = group_done(b, f, late)
                if not group:
                    return
                dve.wait_ge(place_ready, group)
                dve.wait_ge(dve_own, reached["kept"])
                v.tensor_reduce(denom[:, 0:n], kept[:, 0:n], AX, ALU.add)
                v.tensor_tensor(placed[:, 0:n], place[:, 0:n].unsqueeze(2).broadcast_to([P, n, K, E]), onehot[:, 0:n],
                                ALU.mult).then_inc(dve_own, 1)
                reached["placed"] = own.next()

            def slot_rows(b, f=1, late=False):
                group, n = group_done(b, f, late)
                if not group:
                    return
                dve.wait_ge(dve_own, reached["placed"])
                weight = xrow[:, :, TPB * (b + 1) - n:TPB * (b + 1), C + 1].rearrange("p k t -> p t k")
                v.reciprocal(weight, denom[:, 0:n])
                with nc.allow_low_precision(reason="one whole number of each eight is not zero"):
                    v.tensor_reduce(slot[:, TPB * (b + 1) - n:TPB * (b + 1), :], placed[:, 0:n], AX, ALU.add)\
                        .then_inc(slot_ready, 1)

            def slots(f, ends, less, shift, first, n):
                past_n, past_tiles_n = past[:, 0:n, :], past_tiles[:, 0:n, :]
                v.tensor_tensor(past_n, ends.unsqueeze(1).broadcast_to([1, n, E]),
                                iota_s[:, 0:n].unsqueeze(2).broadcast_to([1, n, E]), ALU.is_le).then_inc(dve_own, 1)
                dve.wait_ge(dve_own, own.next())
                v.tensor_tensor(past_tiles_n, past_n, less.unsqueeze(1).broadcast_to([1, n, E]), ALU.mult)
                v.tensor_reduce(expert_f[:, 0:n], past_n, AX, ALU.add).then_inc(dve_own, 1)
                dve.wait_ge(dve_own, own.next())
                v.tensor_reduce(first_of[:, 0:n], past_tiles_n, AX, ALU.add)
                v.scalar_tensor_tensor(row_a[:, 0:n], expert_f[:, 0:n], float(REG), shift, ALU.mult, ALU.add)
                v.tensor_scalar(expert_tab[:, f, first:first + n], expert_f[:, 0:n], float(E - 1), None, ALU.min)\
                    .then_inc(dve_own, 1)
                dve.wait_ge(dve_own, own.next())
                v.scalar_tensor_tensor(row_tab[:, f, first:first + n], first_of[:, 0:n], float(-P), row_a[:, 0:n],
                                       ALU.mult, ALU.add).then_inc(tables_ready, 1)

            def early_counts(b, f=1):
                if b == HALF - 1:
                    dve.wait_ge(count_ready, 2 * f + 1)
                    v.tensor_copy(count[:], count_ps[0:1, :]).then_inc(count_copied, 1)

            def early_tables(b, f=1):
                if b != HALF - 1:
                    return
                dve.wait_ge(count_copied, 2 * f + 1)
                dve.wait_ge(consts_ready, 2)
                v.tensor_tensor(over[:, :, 1:NT], thresholds[:, :, 1:NT],
                                count[:].unsqueeze(2).broadcast_to([1, E, NT - 1]), ALU.is_le).then_inc(dve_own, 1)
                dve.wait_ge(dve_own, own.next())
                v.tensor_reduce(tiles_of[:], over[:, :, 1:NT], AX, ALU.add).then_inc(dve_own, 1)
                dve.wait_ge(dve_own, own.next())
                v.tensor_tensor_scan(tiles_end[:], ones_e[:], tiles_of[:], 0.0, ALU.mult, ALU.add).then_inc(dve_own, 1)
                dve.wait_ge(dve_own, own.next())
                v.tensor_scalar(early_end[:], tiles_end[:], float(EARLY), None, ALU.min)
                slots(f, tiles_end[:], tiles_of[:], iota_s128[:, 0:EARLY], 0, EARLY)

            def late_tables(f, part):
                late = NS - EARLY
                if part == 0:
                    dve.wait_ge(count_ready, 2 * f + 2)
                    v.tensor_copy(count[:], count_ps[0:1, :]).then_inc(count_copied, 1)
                    v.tensor_copy(early_of[:, 0:1], early_end[:, 0:1])
                    v.tensor_tensor(early_of[:, 1:E], early_end[:, 1:E], early_end[:, 0:E - 1], ALU.subtract)
                    v.memset(early_of[:, E:E + 1], 0.0).then_inc(dve_own, 1)
                    dve.wait_ge(count_copied, 2 * f + 2)
                    v.tensor_tensor(pad_tab[:, f, :], count[:], region[0:1, :], ALU.add).then_inc(tables_ready, 1)
                    v.tensor_tensor(over[:], thresholds[:], count[:].unsqueeze(2).broadcast_to([1, E, NT]),
                                    ALU.is_lt).then_inc(dve_own, 1)
                    dve.wait_ge(dve_own, own.next())
                    v.tensor_tensor(early_step[:], early_of[:, 1:E + 1], early_of[:, 0:E], ALU.subtract)
                    v.scalar_tensor_tensor(late_start[:, 0:late], early_of[:, 0:1].broadcast_to([1, late]), float(P),
                                           iota_s128[:, 0:late], ALU.mult, ALU.add)
                    dve.wait_ge(dve_own, own.next())
                    v.tensor_reduce(tiles_of[:], over[:], AX, ALU.add).then_inc(dve_own, 1)
                if part == 1:
                    dve.wait_ge(dve_own, own.next())
                    v.tensor_tensor(tiles_of[:], tiles_of[:], early_of[:, 0:E], ALU.subtract).then_inc(dve_own, 1)
                    dve.wait_ge(dve_own, own.next())
                    v.tensor_tensor(skipped[:], tiles_of[:], early_step[:], ALU.subtract)
                    v.tensor_tensor_scan(tiles_end[:], ones_e[:], tiles_of[:], 0.0, ALU.mult, ALU.add)\
                        .then_inc(dve_own, 1)
                    dve.wait_ge(dve_own, own.next())
                    v.tensor_scalar(used_tab[:, f:f + 1], tiles_end[:, E - 1:E], float(EARLY), None, ALU.add)
                if part == 2:
                    slots(f, tiles_end[:], skipped[:], late_start[:, 0:late], EARLY, late)

            def experts(f):
                def x_lo(g, c):
                    s = c % RING
                    dve.wait_ge(xg_loaded[f][s], (g + (c // RING + 1)) * 16)
                    if not (isinstance(g, int) and c < RING):
                        dve.wait_ge(y_scattered[f][s], (g + c // RING) * 16)
                    v.tensor_copy(result_row[:, s:s + 1], xg[:, s, C:C + 1])
                    v.tensor_copy(row_weight[:, s:s + 1], xg[:, s, C + 1:C + 2])
                    dve.wait_ge(xT_hi_ready[f], g * RING + (c + 1))
                    v.tensor_tensor(xT_lo[:, c % PR, :], xT_ps, xT_hi[:, c % PR, :].bitcast(F32),
                                    ALU.subtract).then_inc(xT_lo_ready[f], 1)

                def products(g, c):
                    dve.wait_ge(silu_ready[f], g * RING + (c + 1))
                    dve.wait_ge(up_ps_ready[f], g * RING + (c + 1))
                    v.tensor_tensor(h[:, c % PR, :], up_ps[c % PB][:], silu[:, c % PR, :], ALU.mult)\
                        .then_inc(h_ready[f], 1)

                def step(g, c):
                    alone = isinstance(g, int)
                    if alone and c == 0:
                        x_lo(0, 0)
                        route_top(NB - 1, f, late=True)
                        x_lo(0, 1)
                        route_choose(NB - 1, f, late=True)
                        products(0, 0)
                    if not alone or c + 2 < NS:
                        x_lo(g, c + 2)
                    if alone and c == 0:
                        route_count(NB - 1, f, late=True)
                        place_rows(NB - 1, f, late=True)
                        place_sums(NB - 1, f, late=True)
                    if not alone or c + 1 < NS:
                        products(g, c + 1)
                    if not alone or c >= 1:
                        s = (c - 1) % RING
                        dve.wait_ge(y_ps_ready[f], g * RING + c)
                        v.tensor_scalar(y[:, s, :], y_ps, row_weight[:, s:s + 1], None, ALU.mult)\
                            .then_inc(y_ready[f], 1)
                    if alone and c == 0:
                        slot_rows(NB - 1, f, late=True)
                    if alone and LATE_AT <= c < LATE_AT + 3:
                        late_tables(f, c - LATE_AT)
                loop_tiles(dve, f, step)

            def span(b):
                return slice(TPB * b, TPB * (b + 1))

            def y_sum(b, f=0):
                dve.wait_ge(y_loaded[b], 16 * (f + 1))
                v.tensor_tensor(Y[:, span(b), 0, :], Y[:, span(b), 0, :], Y[:, span(b), 1, :], ALU.add)\
                    .then_inc(y_sum_ready, 1)

            def x_and_experts(b, f=0):
                dve.wait_ge(y_sum_ready, NB * f + b + 1)
                v.scalar_tensor_tensor(X[:, span(b), :], Y[:, span(b), 0, :], 0.5, X[:, span(b), :], ALU.mult, ALU.add)\
                    .then_inc(x2_ready, 1)

            dve.wait_ge(consts_ready, 1)
            def w13_rest(e):
                dve.wait_ge(w13_hi_ready, e + 1)
                for i in range(2):
                    last = v.tensor_tensor(w13_lo[:, e, i, :], w13_raw[:, e, i, :], w13_hi[:, e, i, :].bitcast(F32),
                                           ALU.subtract)
                last.then_inc(w13_lo_ready, 1)

            loads = [slice(TL * n, TL * (n + 1)) for n in range(NL)]
            for n in range(NL):
                dve.wait_ge(x_loaded[n], 16)
                stats_of(loads[n], stats, mv, var_eps, var_ready)
                if n >= 1:
                    dve.wait_ge(rstd_ready, n)
                    shift_of(loads[n - 1], mv, rstd, shift, shift_ready)
            dve.wait_ge(rstd_ready, NL)
            shift_of(loads[NL - 1], mv, rstd, shift, shift_ready)
            pipeline(
                (lambda b: early_counts(b, 0), 3), (lambda b: slot_rows(b, 0), 3), (w13_rest, 7),
                (lambda b: route_top(b, 0), 2), (lambda b: route_choose(b, 0), 2),
                (lambda b: route_count(b, 0), 2), (lambda b: early_tables(b, 0), 3),
                (lambda b: copy_rows(b, 0), 0), (lambda b: place_rows(b, 0), 2),
                (lambda b: place_sums(b, 0), 2)
            )
            experts(0)

            def tiles_of_batch(b):
                return range(TPB * b, TPB * (b + 1))

            def x2_stats(b):
                dve.wait_ge(x2_ready, b + 1)
                for t in tiles_of_batch(b):
                    last = v.bn_stats(stats2[:, t, :], X[:, t, :])
                last.then_inc(stats2_ready, 1)

            def x2_mean(b):
                dve.wait_ge(stats2_ready, b + 1)
                for t in tiles_of_batch(b):
                    last = v.bn_aggr(mv2[:, t, :], stats2[:, t, :])
                last.then_inc(mean2_ready, 1)

            def x2_var(b):
                dve.wait_ge(mean2_ready, b + 1)
                v.tensor_scalar(var_eps2[:, span(b)], mv2[:, span(b), 1], EPS_LN, None, ALU.add).then_inc(var2_ready, 1)

            def x2_shift(b):
                dve.wait_ge(rstd2_ready, b + 1)
                shift_of(span(b), mv2, rstd2, shift2, shift2_ready)

            def kv_mask(b):
                dve.wait_ge(kvo_ps_ready, b + 1)
                if b >= 2:
                    dve.wait_ge(att_ps_ready, b - 1)
                v.tensor_tensor(kv[:, b % 2, :], kvo_ps, head_mask[:], ALU.mult).then_inc(kv_ready, 1)

            def att_den(b):
                dve.wait_ge(att_ps_ready, b + 1)
                v.tensor_scalar(den[:, b % 2, :, :], att_ps[:, :, C:VW], EPS_ATTN, None, ALU.add).then_inc(den_ready, 1)

            def att_rden(b):
                dve.wait_ge(den_ready, b + 1)
                v.reciprocal(rden[:, b % 2, :, :], den[:, b % 2, :, :]).then_inc(rden_ready, 1)

            def att_div(b):
                dve.wait_ge(rden_ready, b + 1)
                if b >= 2:
                    dve.wait_ge(attT_ps_ready, b - 1)
                v.tensor_tensor(att[:, b % 2, :, :].rearrange("p t (h d) -> p t h d", h=HEADS),
                                att_ps[:, :, 0:C].rearrange("p t (h d) -> p t h d", h=HEADS),
                                rden[:, b % 2, :, :].unsqueeze(3).broadcast_to([P, TPB, HEADS, D]),
                                ALU.mult).then_inc(att_ready, 1)

            def x3(b):
                dve.wait_ge(proj_ps_ready, b + 1)
                v.tensor_tensor(X[:, span(b), :], proj_ps, X[:, span(b), :], ALU.add).then_inc(x3_ready, 1)

            def x3_stats(b):
                dve.wait_ge(x3_ready, b + 1)
                for t in tiles_of_batch(b):
                    last = v.bn_stats(stats[:, t, :], X[:, t, :])
                last.then_inc(stats_ready, 1)

            def x3_mean(b):
                dve.wait_ge(stats_ready, b + 1)
                for t in tiles_of_batch(b):
                    last = v.bn_aggr(mv[:, t, :], stats[:, t, :])
                last.then_inc(mean_ready, 1)

            def x3_var(b):
                dve.wait_ge(mean_ready, b + 1)
                v.tensor_scalar(var_eps[:, span(b)], mv[:, span(b), 1], EPS_LN, None, ALU.add).then_inc(var_ready, 1)

            def x3_shift(b):
                dve.wait_ge(rstd_ready, NL + b + 1)
                shift_of(span(b), mv, rstd, shift, shift_ready)

            pipeline(
                (att_div, 6), (x3_stats, 7), (place_sums, 10), (x3_mean, 7), (x2_mean, 2),
                (x_and_experts, 1), (slot_rows, 10), (x3_shift, 8), (x3_var, 7), (x2_var, 2),
                (early_tables, 11), (copy_rows, 9), (route_top, 9), (kv_mask, 5), (y_sum, 0),
                (x2_stats, 1), (route_choose, 9), (x3, 6), (route_count, 9), (early_counts, 10),
                (att_den, 5), (x2_shift, 2), (att_rden, 5), (place_rows, 9)
            )
            experts(1)
            pipeline((lambda b: y_sum(b, 1), 0), (lambda b: x_and_experts(b, 1), 1))

        @block.tensor
        def _(pe):
            mm = nc.tensor.matmul

            written = {"xnT": 0, "xn2T": 0, "scores": 0, "ranks": 0, "counts": 0}

            def xn_transposes(b, f=1):
                pe.wait_ge(xn_ready, NB * f + b + 1)
                if written["xnT"]:
                    pe.wait_ge(xnT_ready, written["xnT"])
                if written["xn2T"]:
                    pe.wait_ge(xn2T_ready, written["xn2T"])
                for j in range(TPB):
                    last = nc.tensor.transpose(xnT_ps[:, j * P:(j + 1) * P], xrow[:, 0, TPB * b + j, 0:C], ident[:])
                last.then_inc(xnT_ps_ready, 1)
                written["xnT"] += 1

            def scores(b, f=1):
                pe.wait_ge(xnT_ready, NB * f + b + 1)
                if written["scores"]:
                    pe.wait_ge(S_ready, written["scores"])
                if written["ranks"]:
                    pe.wait_ge(place_ready, written["ranks"])
                if written["counts"]:
                    pe.wait_ge(count_copied, written["counts"])
                for j in range(TPB):
                    last = mm(scores_ps[:, TPB * b + j, :], xnT[:, b % 2, j * P:(j + 1) * P], wgate_sb[:],
                              start=True, stop=True)
                last.then_inc(scores_ready, 1)
                if group_done(b, f)[0]:
                    written["scores"] += 1

            def ranks(b, f=1, late=False):
                group, n = group_done(b, f, late)
                if not group:
                    return
                pe.wait_ge(chosen_ready, group)
                if group > 1:
                    pe.wait_ge(carry_ready, group - 1)
                pe.wait_ge(S_ready, written["scores"])
                if written["ranks"]:
                    pe.wait_ge(place_ready, written["ranks"])
                if written["counts"]:
                    pe.wait_ge(count_copied, written["counts"])
                mm(rank_ps[:, 0:n, :], before[:], chosen[:, 0:n, :], start=True, stop=False)
                for j in range(n - 1):
                    mm(rank_ps[:, j + 1:n, :], ones_b[:],
                       chosen[:, j:j + 1, :].broadcast_to([P, n - 1 - j, E]), start=False, stop=False)
                done = b + 1 - n // TPB
                mm(rank_ps[:, 0:n, :], ones_b[:], carry[:, done:done + 1, :].broadcast_to([P, n, E]),
                   start=False, stop=True).then_inc(rank_ready, 1)
                written["ranks"] += 1

            def counts(b, f=1, late=False):
                if b != (NB if late else HALF) - 1:
                    return
                pe.wait_ge(carry_ready, group_done(b, f)[0])
                pe.wait_ge(place_ready, written["ranks"])
                pe.wait_ge(S_ready, written["scores"])
                mm(count_ps, ones_b[:], carry[:, b + 1, :], start=True, stop=True).then_inc(count_ready, 1)
                written["counts"] += 1

            def experts(f):
                def expert_of(g, c):
                    return nc.tensor.value_load(expert_tab[0:1, f, bass.ds(g * RING + c, 1)], min_val=0, max_val=E - 1)

                def x_transpose(g, c):
                    s = c % RING
                    pe.wait_ge(xg_loaded[f][s], (g + (c // RING + 1)) * 16)
                    if not (isinstance(g, int) and c == 0):
                        pe.wait_ge(xT_lo_ready[f], g * RING + c)
                    nc.tensor.transpose(xT_ps, xg[:, s, 0:C], ident[:]).then_inc(xT_ps_ready[f], 1)

                def up(g, c):
                    s = c % PR
                    if isinstance(g, int) and c == EARLY:
                        pe.wait_ge(tables_ready, 3 * f + 3)
                    e = expert_of(g, c)
                    pe.wait_ge(xT_lo_ready[f], g * RING + (c + 1))
                    halves = (gate_ps[c % PB], gate_ps_ready[f]), (up_ps[c % PB], up_ps_ready[f])
                    for i, (ps, ready) in enumerate(halves):
                        mm(ps[:], xT_hi[:, s, :], w13_hi[:, bass.ds(e, 1), i, :], start=True, stop=False)
                        mm(ps[:], xT_hi[:, s, :], w13_lo[:, bass.ds(e, 1), i, :], start=False, stop=False)
                        mm(ps[:], xT_lo[:, s, :], w13_hi[:, bass.ds(e, 1), i, :], start=False, stop=True)\
                            .then_inc(ready, 1)

                def down(g, c):
                    e = expert_of(g, c)
                    pe.wait_ge(hT_ready[f], g * RING + (c + 1))
                    if not (isinstance(g, int) and c == 0):
                        pe.wait_ge(y_ready[f], g * RING + c)
                    for j in range(FC):
                        last = mm(y_ps, hT[:, c % PR, j * P:(j + 1) * P], w2_sb[:, bass.ds(e, 1), j, :],
                                  start=(j == 0), stop=(j == FC - 1))
                    last.then_inc(y_ps_ready[f], 1)

                def step(g, c):
                    alone = isinstance(g, int)
                    if alone and c == 0:
                        x_transpose(0, 0)
                        x_transpose(0, 1)
                        up(0, 0)
                        ranks(NB - 1, f, late=True)
                    if not alone or c + 2 < NS:
                        x_transpose(g, c + 2)
                    if not alone or c + 1 < NS:
                        up(g, c + 1)
                    if alone and c == 0:
                        counts(NB - 1, f, late=True)
                    if not alone or c >= 1:
                        down(g, c - 1)
                    if not alone or c < NS:
                        pe.wait_ge(h_ready[f], g * RING + (c + 1))
                        for j in range(FC):
                            last = nc.tensor.transpose(hT_ps[:, j * P:(j + 1) * P], h[:, c % PR, j * P:(j + 1) * P],
                                                       ident[:])
                        last.then_inc(hT_ps_ready[f], 1)

                pe.wait_ge(tables_ready, 3 * f + 1)
                loop_tiles(pe, f, step)

            pe.wait_ge(consts_ready, 1)
            pe.wait_ge(wgate_loaded, 16)
            pipeline(
                (lambda b: scores(b, 0), 2), (lambda b: ranks(b, 0), 2), (lambda b: counts(b, 0), 2),
                (lambda b: xn_transposes(b, 0), 0)
            )
            pe.wait_ge(w13_lo_ready, E)
            pe.wait_ge(w2_loaded, 16)
            experts(0)


            def xn2_transposes(b):
                pe.wait_ge(xn2_ready, b + 1)
                pe.wait_ge(xnT_ready, written["xnT"])
                if written["xn2T"]:
                    pe.wait_ge(xn2T_ready, written["xn2T"])
                for j in range(TPB):
                    last = nc.tensor.transpose(xn2T_ps[:, j * P:(j + 1) * P], xn2[:, b % 2, j, :], ident[:])
                last.then_inc(xn2T_ps_ready, 1)
                written["xn2T"] += 1

            def kv_in(b):
                pe.wait_ge(xn2T_ready, b + 1)
                if b:
                    pe.wait_ge(kv_in_ready, b)
                for j in range(TPB):
                    last = mm(kv_ps[:, j, :], xn2T[:, b % 2, j * P:(j + 1) * P], wqkv_sb[:, C:3 * C],
                              start=True, stop=True)
                last.then_inc(kv_ps_ready, 1)

            def q_in(b):
                pe.wait_ge(xn2T_ready, b + 1)
                if b:
                    pe.wait_ge(q_ready, b)
                mm(q_ps, wqkv_sb[:, 0:C], xn2T[:, b % 2, :], start=True, stop=True).then_inc(q_ps_ready, 1)

            def kv_sum(b):
                pe.wait_ge(kv_in_ready, b + 1)
                if b:
                    pe.wait_ge(kv_ready, b)
                for j in range(TPB):
                    last = mm(kvo_ps, kk[:, b % 2, j, :], vv[:, b % 2, j, :], start=(j == 0), stop=(j == TPB - 1))
                last.then_inc(kvo_ps_ready, 1)

            def attend(b):
                pe.wait_ge(q_ready, b + 1)
                pe.wait_ge(kv_ready, b + 1)
                if b:
                    pe.wait_ge(att_ready, b)
                for j in range(TPB):
                    last = mm(att_ps[:, j, :], qT[:, b % 2, j * P:(j + 1) * P], kv[:, b % 2, :], start=True, stop=True)
                last.then_inc(att_ps_ready, 1)

            def att_transposes(b):
                pe.wait_ge(att_ready, b + 1)
                if b:
                    pe.wait_ge(attT_ready, b)
                for j in range(TPB):
                    last = nc.tensor.transpose(attT_ps[:, j * P:(j + 1) * P], att[:, b % 2, j, :], ident[:])
                last.then_inc(attT_ps_ready, 1)

            def project(b):
                pe.wait_ge(attT_ready, b + 1)
                if b:
                    pe.wait_ge(x3_ready, b)
                for j in range(TPB):
                    mm(proj_ps[:, j, :], attT[:, b % 2, j * P:(j + 1) * P], wproj_sb[:], start=True, stop=False)
                    last = mm(proj_ps[:, j, :], ones_f[:], bproj_sb[:], start=False, stop=True)
                last.then_inc(proj_ps_ready, 1)

            pe.wait_ge(wattn_loaded, 48)
            pipeline(
                (scores, 5), (xn2_transposes, 0), (att_transposes, 2), (q_in, 1), (kv_sum, 1), (counts, 6),
                (project, 2), (attend, 1), (xn_transposes, 4), (ranks, 5), (kv_in, 0)
            )
            experts(1)


def kernel(L0_attn_x, L0_attn_W_qkv, L0_attn_W_proj, L0_attn_b_proj, L0_ffn_gate_w, L0_ffn_w1, L0_ffn_w2, L0_ffn_w3):
    import numpy as np
    import concourse.bacc as bacc
    from concourse.bass_utils import run_bass_kernel_spmd

    def laid(a):
        return np.ascontiguousarray(a)

    inputs = {
        "x": laid(np.asarray(L0_attn_x).reshape(NT, P, C).transpose(1, 0, 2)),
        "w_qkv": laid(np.asarray(L0_attn_W_qkv).T),
        "w_proj": laid(np.asarray(L0_attn_W_proj).T),
        "b_proj": laid(np.asarray(L0_attn_b_proj).reshape(1, C)),
        "w_gate": laid(np.asarray(L0_ffn_gate_w).T),
        "w1": laid(np.asarray(L0_ffn_w1).transpose(2, 0, 1)),
        "w3": laid(np.asarray(L0_ffn_w3).transpose(2, 0, 1)),
        "w2": laid(np.asarray(L0_ffn_w2).transpose(2, 0, 1).reshape(FC, P, E, C).transpose(1, 2, 0, 3)),
    }
    nc = bacc.Bacc("TRN2", target_bir_lowering=False, num_devices=1)
    args = [nc.dram_tensor(f"{name}_in", a.shape, F32, kind="ExternalInput").ap() for name, a in inputs.items()]
    out = nc.dram_tensor("out", (P, NT, C), F32, kind="ExternalOutput").ap()
    build(nc, *args, out)
    r = run_bass_kernel_spmd(nc, [{f"{name}_in": a for name, a in inputs.items()}], core_ids=[0])
    return np.ascontiguousarray(r.results[0]["out"].transpose(1, 0, 2)).reshape(NB, TB, C)
```
